# Optimizing a Trainium2 kernel written in Bass

```python
import numpy as np
import jax
import jax.numpy as jnp

def _softmax(x, axis=-1):
    return jax.nn.softmax(x, axis=axis)

def _gelu(x):
    return jax.nn.gelu(x, approximate=True)

def _silu(x):
    return jax.nn.silu(x)

def _sigmoid(x):
    return jax.nn.sigmoid(x)

def _layernorm(x, axis=-1, eps=1e-05):
    m = jnp.mean(x, axis=axis, keepdims=True)
    v = jnp.var(x, axis=axis, keepdims=True)
    return (x - m) / jnp.sqrt(v + eps)

def _scatter_add(tgt, idx, src, axis=0):
    return tgt.at[idx].add(src)

def _segment_sum(src, seg, n):
    return jax.ops.segment_sum(src, seg, n)
kernel_name = 'mk_conv_preact_d1_conv_nchw64_r2_bae7de'

def setup_inputs(seed: int=0):
    np.random.seed(seed)
    _w = jnp.asarray

    def _rec_inputs():
        import jax
        import jax.numpy as jnp
        _gk = jax.random.key(seed)
        x = -9.26e-05 + 0.9999 * jax.random.normal(jax.random.fold_in(_gk, 1), (16, 32, 96, 96), jnp.float32)
        return x
    x = _rec_inputs()

    def _L0_conv_setup():
        import jax, jax.numpy as jnp
        import numpy as np
        NUM_FEAT = 32
        N_EXPERTS = 7
        RES_SCALE = 1.0

        def _conv2d_same(x_nchw, w_oihw, b):
            y = jax.lax.conv_general_dilated(x_nchw, w_oihw, window_strides=(1, 1), padding='SAME', dimension_numbers=('NCHW', 'OIHW', 'NCHW'))
            return y + b[None, :, None, None]
        key = jax.random.key(seed)
        ks = jax.random.split(key, 12)
        B, C, H, W = (16, NUM_FEAT, 96, 96)
        s = 0.05
        inp = {'x': jax.random.normal(ks[0], (B, C, H, W), jnp.float32), 'conv1_w': jax.random.normal(ks[1], (C, C, 3, 3), jnp.float32) * s, 'conv1_b': jax.random.normal(ks[2], (C,), jnp.float32) * s, 'conv2_w': jax.random.normal(ks[3], (C, C, 3, 3), jnp.float32) * s, 'conv2_b': jax.random.normal(ks[4], (C,), jnp.float32) * s, 'experts_w1': jax.random.normal(ks[5], (N_EXPERTS, C, C, 3, 3), jnp.float32) * s, 'experts_b1': jax.random.normal(ks[6], (N_EXPERTS, C), jnp.float32) * s, 'experts_w2': jax.random.normal(ks[7], (N_EXPERTS, C, C, 3, 3), jnp.float32) * s, 'experts_b2': jax.random.normal(ks[8], (N_EXPERTS, C), jnp.float32) * s, 'gate_w': jax.random.normal(ks[9], (N_EXPERTS, C), jnp.float32) * (1.0 / np.sqrt(C)), 'gate_b': jax.random.normal(ks[10], (N_EXPERTS,), jnp.float32) * 0.01}
        return inp
    _L0_conv_all = _L0_conv_setup()
    _L0_conv_in = {k: v for k, v in _L0_conv_all.items() if k in ('conv1_w', 'conv1_b', 'conv2_w', 'conv2_b', 'experts_w1', 'experts_b1', 'experts_w2', 'experts_b2', 'gate_w', 'gate_b')}
    del _L0_conv_all
    return {'x': x, 'L0_conv_conv1_w': _L0_conv_in['conv1_w'], 'L0_conv_conv1_b': _L0_conv_in['conv1_b'], 'L0_conv_conv2_w': _L0_conv_in['conv2_w'], 'L0_conv_conv2_b': _L0_conv_in['conv2_b'], 'L0_conv_experts_w1': _L0_conv_in['experts_w1'], 'L0_conv_experts_b1': _L0_conv_in['experts_b1'], 'L0_conv_experts_w2': _L0_conv_in['experts_w2'], 'L0_conv_experts_b2': _L0_conv_in['experts_b2'], 'L0_conv_gate_w': _L0_conv_in['gate_w'], 'L0_conv_gate_b': _L0_conv_in['gate_b']}

def reference(x, L0_conv_conv1_w, L0_conv_conv1_b, L0_conv_conv2_w, L0_conv_conv2_b, L0_conv_experts_w1, L0_conv_experts_b1, L0_conv_experts_w2, L0_conv_experts_b2, L0_conv_gate_w, L0_conv_gate_b):
    import jax
    import jax.numpy as jnp

    def _L0_conv_ref(x, conv1_w, conv1_b, conv2_w, conv2_b, experts_w1, experts_b1, experts_w2, experts_b2, gate_w, gate_b):
        import jax, jax.numpy as jnp
        import numpy as np
        NUM_FEAT = 32
        N_EXPERTS = 7
        RES_SCALE = 1.0

        def _conv2d_same(x_nchw, w_oihw, b):
            y = jax.lax.conv_general_dilated(x_nchw, w_oihw, window_strides=(1, 1), padding='SAME', dimension_numbers=('NCHW', 'OIHW', 'NCHW'))
            return y + b[None, :, None, None]
        identity = x
        pooled = x.mean(axis=(-2, -1))
        gate = jax.nn.softmax(pooled @ gate_w.T + gate_b)
        kw1 = jnp.einsum('be,eoihw->boihw', gate, experts_w1) + conv1_w
        kb1 = gate @ experts_b1 + conv1_b
        kw2 = jnp.einsum('be,eoihw->boihw', gate, experts_w2) + conv2_w
        kb2 = gate @ experts_b2 + conv2_b
        per_sample = jax.vmap(lambda xi, wi, bi: _conv2d_same(xi[None], wi, bi)[0])
        out1 = jax.nn.relu(per_sample(x, kw1, kb1))
        out2 = per_sample(out1, kw2, kb2)
        return identity + out2 * RES_SCALE

    def _gn(v, G=32, eps=1e-05):
        B_, C_, H_, W_ = v.shape
        g = v.reshape(B_, G, C_ // G, H_, W_)
        m = jnp.mean(g, axis=(2, 3, 4), keepdims=True)
        s = jnp.var(g, axis=(2, 3, 4), keepdims=True)
        return ((g - m) / jnp.sqrt(s + eps)).reshape(v.shape)

    def _ln_c(v, eps=1e-06):
        m = jnp.mean(v, axis=1, keepdims=True)
        s = jnp.var(v, axis=1, keepdims=True)
        return (v - m) / jnp.sqrt(s + eps)

    def _ln_t(v, eps=1e-05):
        m = jnp.mean(v, axis=-1, keepdims=True)
        s = jnp.var(v, axis=-1, keepdims=True)
        return (v - m) / jnp.sqrt(s + eps)

    def _to_tokens(v):
        B_, C_, H_, W_ = v.shape
        return v.reshape(B_, C_, H_ * W_).transpose(0, 2, 1)

    def _from_tokens(t, like):
        B_, C_, H_, W_ = like.shape
        return t.transpose(0, 2, 1).reshape(B_, C_, H_, W_)
    x = x + _L0_conv_ref(_gn(x), L0_conv_conv1_w, L0_conv_conv1_b, L0_conv_conv2_w, L0_conv_conv2_b, L0_conv_experts_w1, L0_conv_experts_b1, L0_conv_experts_w2, L0_conv_experts_b2, L0_conv_gate_w, L0_conv_gate_b)
    return x

_drawn_inputs = setup_inputs


def setup_inputs(seed=0):
    import zlib

    import numpy as np

    out = dict(_drawn_inputs(seed))
    spreads = {}
    factors = {'L0_conv_conv1_b': 3.598,
     'L0_conv_experts_b1': 8.0,
     'L0_conv_experts_b2': 5.905,
     'L0_conv_gate_w': 64.0,
     'L0_conv_gate_b': 36.976}
    for name, (base, spread) in spreads.items():
        noise = np.random.default_rng([zlib.crc32(name.encode()), seed]).standard_normal(out[name].shape)
        drawn = base * np.exp(spread * noise) if base else spread * noise
        out[name] = jnp.asarray(drawn.astype(out[name].dtype))
    for name, factor in factors.items():
        out[name] = (out[name] * factor).astype(out[name].dtype)
    return out
```

```python
from contextlib import ExitStack

import concourse.bass as bass
from concourse import mybir

F32 = mybir.dt.float32
F16 = mybir.dt.float16
ALU = mybir.AluOpType
ACT = mybir.ActivationFunctionType
AX_X = mybir.AxisListType.X

P = 128
EPS = 1e-5
WS = 16.0
HS = 0.25
STRAIGHT, CROSSED = 0, 1
HI, LO = 0, 1
PRODUCTS = ((HI, HI), (LO, HI), (HI, LO))


class Sample:

    def __init__(self, i, c):
        self.i, self.c = i, c

    def plus(self, n):
        return Sample(self.i, self.c + n)

    @property
    def number(self):
        return self.i * 2 + self.c

    @property
    def parity(self):
        return self.c % 2

    @property
    def pair(self):
        return self.i + self.c // 2

    def known(self, value):
        return isinstance(self.i, int) and self.i * 2 + self.c == value

    def at_least(self, value):
        return self.c >= value


def build(nc, x, w1, b1, w2, b2, ew1, eb1, ew2, eb2, gw, gb, out):
    N, C, H, W = x.shape
    E = ew1.shape[0]
    G = P // C
    NB = H // G
    NS = NB + 1
    RP = W + 2
    GRP = 5
    SPG = NS // GRP
    PIX = NB * W
    TAPS = 3 * 2 * C
    E1 = E + 1
    assert G == 4 and NS == GRP * SPG and SPG * W <= 512 and E1 == 8
    STAT = 6
    SC = PIX // STAT
    LOAD = 16 * G

    ctx = ExitStack()
    with ctx:
        def sb(name, shape, dt=F32):
            return ctx.enter_context(nc.sbuf_tensor(name, shape, dt))

        def sem(name):
            return ctx.enter_context(nc.semaphore(name))

        xin = [sb(f"xin{i}", [P, NB, W]) for i in range(2)]
        res = [sb(f"res{i}", [P, NB, W]) for i in range(2)]
        xh = sb("xh", [P, NB, W])
        a1 = [sb(f"a1_{i}", [P, 2, NB, RP], F16) for i in range(2)]
        c1 = [sb(f"c1_{i}", [P, 2, NS, RP], F16) for i in range(2)]
        a2 = [sb(f"a2_{i}", [P, 2, NS, RP], F16) for i in range(2)]
        c2 = [sb(f"c2_{i}", [P, 2, NB, RP], F16) for i in range(2)]
        hid = [sb(f"hid{i}", [P, SPG, W]) for i in range(2)]
        natural = sb("natural", [P, 2, 2, C * 9])
        padded = sb("padded", [P, 2, 2, 3, 5, C])
        bank = sb("bank", [P, E1, 2, TAPS + 1])
        mix = sb("mix", [P, 2, 2, TAPS + 1])
        wts = [[sb(f"wts{i}_{k}", [P, 2, 2, TAPS], F16) for k in range(2)] for i in range(2)]
        small = sb("small", [32, G, C])
        table = sb("table", [P, 3 * E + 2])
        gbias = sb("gbias", [P, E])
        ident = sb("ident", [P, P])
        pick = sb("pick", [P, C])
        avg = sb("avg", [P, P])
        ones = sb("ones", [P, P])
        minus_half = sb("minus_half", [P, 1])
        stats = [sb(f"stats{i}", [P, STAT, 6]) for i in range(2)]
        mv = [sb(f"mv{i}", [P, 2]) for i in range(2)]
        col = [sb(f"col{i}", [P, 16]) for i in range(2)]
        logit = [sb(f"logit{i}", [P, E]) for i in range(2)]
        expo = [sb(f"expo{i}", [P, E]) for i in range(2)]
        gwp = [sb(f"gwp{i}", [P, E]) for i in range(2)]
        gate = [sb(f"gate{i}", [P, E]) for i in range(2)]
        DEV, DVAR, VEPS, NMEAN, RSTD, NBIAS, RS1, RB, B1, POOLED, NMAX, ESUM, RSUM = range(13)

        pg = [ctx.enter_context(nc.psum_tensor(f"pg{i}", [P, 512], F32)) for i in range(GRP)]
        pstat = ctx.enter_context(nc.psum_tensor("pstat", [P, 512], F32))
        pgate = ctx.enter_context(nc.psum_tensor("pgate", [P, 512], F32))
        pset = ctx.enter_context(nc.psum_tensor("pset", [P, 512], F32))

        x_in = [sem(f"x_in{i}") for i in range(2)]
        crossed1 = [sem(f"crossed1_{i}") for i in range(2)]
        crossed2 = [sem(f"crossed2_{i}") for i in range(2)]
        stored = [sem(f"stored{i}") for i in range(2)]
        w_in = sem("w_in")
        s_in = sem("s_in")
        ident_ok = sem("ident_ok")
        consts_ok = sem("consts_ok")
        pads_ok = sem("pads_ok")
        small_ok = sem("small_ok")
        table_ps = sem("table_ps")
        padded_ok = sem("padded_ok")
        wt_ps = sem("wt_ps")
        wt_act = sem("wt_act")
        wt_dve = sem("wt_dve")
        bank_ok = sem("bank_ok")
        mv_ok = sem("mv_ok")
        mean_ps = sem("mean_ps")
        dvar_ok = sem("dvar_ok")
        var_ps = sem("var_ps")
        veps_ok = sem("veps_ok")
        coef_ok = sem("coef_ok")
        xh_ok = sem("xh_ok")
        hi1_ok = sem("hi1_ok")
        lo1_ok = sem("lo1_ok")
        gwp_ok = sem("gwp_ok")
        gate_ps = sem("gate_ps")
        logit_ok = sem("logit_ok")
        expo_ok = sem("expo_ok")
        bias_ok = sem("bias_ok")
        mix_ok = sem("mix_ok")
        whi_ok = sem("whi_ok")
        w1_ok = sem("w1_ok")
        w2_ok = sem("w2_ok")
        res_ok = sem("res_ok")
        conv1_ps = sem("conv1_ps")
        hid_ok = sem("hid_ok")
        lo2_ok = sem("lo2_ok")
        conv2_ps = sem("conv2_ps")
        fin_ok = sem("fin_ok")
        dve_link = sem("dve_link")
        pool_link = sem("pool_link")

        class Link:

            def __init__(self, eng, s):
                self.eng, self.sem, self.base, self.n = eng, s, 0, 0

            def __call__(self, ins):
                ins.then_inc(self.sem, 1)
                self.n += 1
                self.eng.wait_ge(self.sem, self.base + self.n)

        def halves(t):
            return t[0:P // 2], t[P // 2:P]

        def slots(g, first=0, last=NS):
            return range(max(g * SPG, first), min((g + 1) * SPG, last))

        def g_parity(s, g):
            return (s.c * GRP + g) % 2

        def group_pieces(g):
            j0, j1 = g * SPG, (g + 1) * SPG
            if g == 0:
                return ((P - C, P, 0, 1), (0, P, 1, j1))
            if g == GRP - 1:
                return ((0, P, j0, j1 - 1), (0, P - C, j1 - 1, j1))
            return ((0, P, j0, j1),)

        LOOP = range(2, N - 2, 2)

        def schedule(eng, slot, link=None, before=0):
            slot(Sample(0, 0))
            slot(Sample(0, 1))
            start = link.n if link else 0
            with eng.Fori(0, len(LOOP)) as i:
                if link:
                    per = before
                    link.base, link.n = i * per + start, 0
                slot(Sample(i, 2))
                slot(Sample(i, 3))
                if link:
                    assert link.n == per, link.n
            if link:
                link.base, link.n = start + per * len(LOOP), 0
            for s in range(N - 2, N + 1):
                slot(Sample(0, s))

        block = ctx.enter_context(nc.Block())

        @block.sync
        def _(sp):
            xv = x.rearrange("n c (k g) w -> n g c k w", g=G)
            ov = out.rearrange("n c (k g) w -> n g c k w", g=G)

            def load(t):
                for g in range(G):
                    sp.dma_start(xin[t.parity][g * C:(g + 1) * C, :, :],
                                 xv[t.number, g]).then_inc(x_in[t.parity], 16)

            def store(t):
                for g in range(G):
                    sp.dma_start(ov[t.number, g],
                                 res[t.parity][g * C:(g + 1) * C, :, :]).then_inc(stored[t.parity], 16)

            load(Sample(0, 0))
            for v, (ew, bw) in enumerate(((ew1, w1), (ew2, w2))):
                kernels = ew.rearrange("e o c h w -> (e o) (c h w)")
                sp.dma_start(natural[:, v, 0, :], kernels[0:P, :]).then_inc(w_in, 16)
                sp.dma_start(natural[0:(E - 4) * C, v, 1, :], kernels[P:E * C, :]).then_inc(w_in, 16)
                sp.dma_start(natural[(E - 4) * C:P, v, 1, :],
                             bw.rearrange("o c h w -> o (c h w)")).then_inc(w_in, 16)
            load(Sample(0, 1))

            def cross(dst, src, half, d0, s0, done):
                sp.dma_start(halves(dst)[half][:, :, d0:d0 + NB, :].rearrange("p a b w -> p a (b w)"),
                             halves(src)[half][:, :, s0:s0 + NB, :].rearrange("p a b w -> p a (b w)")
                             ).then_inc(done, 16)

            def cross1(t):
                sp.wait_ge(lo1_ok, t.number + 1)
                cross(c1[t.parity], a1[t.parity], 0, 0, 0, crossed1[t.parity])
                cross(c1[t.parity], a1[t.parity], 1, 1, 0, crossed1[t.parity])

            def cross2(t):
                sp.wait_ge(lo2_ok, (t.number + 1) * GRP)
                cross(c2[t.parity], a2[t.parity], 0, 0, 1, crossed2[t.parity])
                cross(c2[t.parity], a2[t.parity], 1, 0, 0, crossed2[t.parity])

            cross1(Sample(0, 0))

            def slot(s):
                if not s.at_least(N - 2):
                    sp.wait_ge(res_ok, s.number + 1)
                    load(s.plus(2))
                if not s.at_least(N):
                    cross2(s)
                if not s.at_least(N - 1):
                    cross1(s.plus(1))
                if s.at_least(1):
                    sp.wait_ge(fin_ok, s.number * GRP)
                    store(s.plus(-1))

            schedule(sp, slot)
            for b in range(2):
                sp.wait_ge(stored[b], LOAD * (N // 2))

        @block.tensor
        def _(pe):
            pe.wait_ge(ident_ok, 1)
            pe.wait_ge(small_ok, 1)
            nc.tensor.transpose(pset[:, 0:32], small[:, :, :].rearrange("p g c -> p (g c)"),
                                ident[0:32, 0:32]).then_inc(table_ps, 1)
            pe.wait_ge(padded_ok, 2)
            n = 0
            for v in range(2):
                for eg in range(2):
                    for part in range(2):
                        if n >= 4:
                            pe.wait_ge(wt_act if n % 2 == 0 else wt_dve, (n - 4) // 2 + 1)
                        for j in range(3):
                            kw, row = divmod(part * 3 + j, 2)
                            last = nc.tensor.transpose(
                                pg[n % 4][:, j * P:(j + 1) * P],
                                padded[:, v, eg, kw, 1 - row:5 - row, :].rearrange("p h c -> p (h c)"),
                                ident[:, :])
                        last.then_inc(wt_ps, 1)
                        n += 1

            def mean_over_rows(t):
                pe.wait_ge(mv_ok, t.number + 1)
                nc.tensor.matmul(pstat[:, 0:1], avg[:, :], mv[t.parity][:, 0:1],
                                 start=True, stop=True).then_inc(mean_ps, 1)

            def var_over_rows(t):
                pe.wait_ge(dvar_ok, t.number + 1)
                nc.tensor.matmul(pstat[:, 1:2], avg[:, :], col[t.parity][:, DVAR:DVAR + 1],
                                 start=True, stop=True).then_inc(var_ps, 1)

            def logits(t):
                pe.wait_ge(gwp_ok, t.number + 1)
                nc.tensor.matmul(pgate[:, 0:E], ones[:, :], gwp[t.parity][:, :],
                                 start=True, stop=True).then_inc(gate_ps, 1)

            def group(v, s, left, right, kind_left, kind_right):
                w = [wts[s.parity][k][:, v] for k in (kind_left, kind_right)]
                ps = pg[left[4]]
                for image, weight in PRODUCTS:
                    for kw in range(3):
                        first = (image, weight, kw) == (HI, HI, 0)
                        final = (image, weight, kw) == (*PRODUCTS[-1], 2)
                        for side, (t, b0, nb, at, _) in enumerate((left, right)):
                            last = nc.tensor.matmul(
                                ps[side * 64:side * 64 + 64, at:at + nb * W].rearrange("p (b w) -> p b w", w=W),
                                w[side][:, weight, kw * 64:(kw + 1) * 64],
                                t[:, image, b0:b0 + nb, kw:kw + W],
                                start=first, stop=final)
                return last

            def conv1_group(s, g):
                if s.at_least(2):
                    pe.wait_ge(fin_ok, (s.number - 2) * GRP + g + 1)
                elif s.at_least(1):
                    pe.wait_ge(hid_ok, g + 1)
                lo, hi = g * SPG, (g + 1) * SPG
                skip = 1 if g == 0 else 0
                group(0, s,
                      (a1[s.parity], lo - 1 + skip, SPG - skip, skip * W, g),
                      (c1[s.parity], lo, SPG, 0, g), STRAIGHT, CROSSED).then_inc(conv1_ps, 1)

            def conv2_group(s, g):
                if not s.at_least(N - 1):
                    pe.wait_ge(hid_ok, (s.number + 1) * GRP + g + 1)
                elif g == 0:
                    pass
                n = len(slots(g, 0, NB))
                group(1, s,
                      (c2[s.parity], g * SPG, n, 0, g),
                      (a2[s.parity], g * SPG + 1, n, 0, g), CROSSED, STRAIGHT).then_inc(conv2_ps, 1)

            pre0 = Sample(0, 0)
            mean_over_rows(pre0)
            var_over_rows(pre0)
            logits(pre0)

            def slot(s):
                more = not s.at_least(N - 1)
                for g in range(GRP):
                    if not s.at_least(N):
                        if g == 0:
                            pe.wait_ge(w1_ok, s.number + 1)
                            pe.wait_ge(lo1_ok, s.number + 1)
                            pe.wait_ge(crossed1[s.parity], 32 * (s.pair + 1))
                            if s.known(0):
                                pe.wait_ge(wt_act, 4)
                                pe.wait_ge(wt_dve, 4)
                        conv1_group(s, g)
                    if more and g == 1:
                        mean_over_rows(s.plus(1))
                    if more and g == 2:
                        var_over_rows(s.plus(1))
                for g in range(GRP):
                    if s.at_least(1):
                        if g == 0:
                            pe.wait_ge(w2_ok, s.number)
                            pe.wait_ge(lo2_ok, s.number * GRP)
                            pe.wait_ge(crossed2[s.plus(-1).parity], 32 * (s.plus(-1).pair + 1))
                        if s.at_least(N) :
                            pe.wait_ge(fin_ok, (s.number - 2) * GRP + g + 1)
                        conv2_group(s.plus(-1), g)
                    if more and g == 0:
                        logits(s.plus(1))

            schedule(pe, slot)

        @block.scalar
        def _(act):
            rows = [(gw, 0), (eb1, E), (b1.rearrange("(a c) -> a c", a=1), 2 * E),
                    (eb2, 2 * E + 1), (b2.rearrange("(a c) -> a c", a=1), 3 * E + 1)]
            act.wait_ge(consts_ok, 2)
            for src, r in rows:
                act.dma_start(small[r:r + src.shape[0], 0, :], src).then_inc(s_in, 16)
            act.dma_start(gbias[:, :], gb.rearrange("(a e) -> a e", a=1).to_broadcast([P, E])).then_inc(s_in, 16)
            act.wait_ge(w_in, 16 * 6)
            act.wait_ge(consts_ok, 1)
            for eg in range(2):
                last = nc.scalar.copy(padded[:, 1, eg, :, 1:4, :],
                                      natural[:, 1, eg, :].rearrange("p (c h w) -> p w h c", c=C, h=3))
            last.then_inc(padded_ok, 1)
            for m in range(4):
                n = 2 * m
                v, eg, part = n // 4, n // 2 % 2, n % 2
                act.wait_ge(wt_ps, n + 1)
                nc.scalar.copy(bank[:, 4 * eg:4 * eg + 4, v, part * 96:part * 96 + 96]
                               .rearrange("p e (j o) -> p e j o", j=3),
                               pg[n % 4][:, 0:3 * P].rearrange("p (j e o) -> p e j o", j=3, e=4)).then_inc(wt_act, 1)

            def normalise(t):
                c = col[t.parity]
                act.wait_ge(coef_ok, t.number + 1)
                if t.at_least(1):
                    act.wait_ge(lo1_ok, t.number)
                nc.scalar.activation(xh[:, :, :], xin[t.parity][:, :, :], ACT.Identity,
                                     bias=c[:, NBIAS:NBIAS + 1], scale=c[:, RSTD:RSTD + 1],
                                     accum_out=c[:, POOLED:POOLED + 1]).then_inc(xh_ok, 1)

            def high_part(t):
                c = col[t.parity]
                if t.at_least(2):
                    act.wait_ge(conv1_ps, (t.number - 1) * GRP)
                else:
                    act.wait_ge(pads_ok, 1)
                nc.scalar.activation(a1[t.parity][:, HI, :, 1:1 + W], xin[t.parity][:, :, :], ACT.Identity,
                                     bias=c[:, NBIAS:NBIAS + 1], scale=c[:, RSTD:RSTD + 1]).then_inc(hi1_ok, 1)

            def exponentials(t):
                act.wait_ge(logit_ok, t.number + 1)
                c = col[t.parity]
                nc.scalar.activation(expo[t.parity][:, :], logit[t.parity][:, :], ACT.Exp,
                                     bias=c[:, NMAX:NMAX + 1],
                                     accum_out=c[:, ESUM:ESUM + 1]).then_inc(expo_ok, 1)

            def weights_high(t, v):
                act.wait_ge(mix_ok, t.number + 1)
                if t.at_least(2):
                    act.wait_ge((conv1_ps, conv2_ps)[v], (t.number - 1) * GRP)
                nc.scalar.copy(wts[t.parity][STRAIGHT][:, v, HI, :],
                               mix[:, E % 2, v, 0:TAPS]).then_inc(whi_ok, 1)

            def residual(t):
                c = col[t.parity]
                act.wait_ge(bias_ok, t.number + 1)
                if t.at_least(2):
                    act.wait_ge(stored[t.parity], LOAD * t.pair)
                nc.scalar.activation(res[t.parity][:, :, :], xin[t.parity][:, :, :], ACT.Identity,
                                     bias=c[:, RB:RB + 1], scale=c[:, RS1:RS1 + 1]).then_inc(res_ok, 1)

            def hidden(s, g):
                c = col[s.parity]
                act.wait_ge(conv1_ps, s.number * GRP + g + 1)
                if not (s.known(0) and g < 2):
                    act.wait_ge(lo2_ok, s.number * GRP + g - 1)
                if g == 0 and s.at_least(2):
                    act.wait_ge(conv2_ps, (s.number - 1) * GRP)
                elif g == 0:
                    act.wait_ge(pads_ok, 2)
                pieces = group_pieces(g)
                dst = ((hid[g_parity(s, g)], None), (a2[s.parity], HI))
                for tile, part in dst:
                    for p0, p1, j0, j1 in pieces:
                        n0 = j0 - g * SPG
                        n1 = j1 - g * SPG
                        o = tile[p0:p1, n0:n1, :] if part is None else tile[p0:p1, part, j0:j1, 1:1 + W]
                        last = nc.scalar.activation(
                            o, pg[g][p0:p1, n0 * W:n1 * W].rearrange("p (b w) -> p b w", w=W), ACT.Relu,
                            bias=c[p0:p1, B1:B1 + 1], scale=HS / WS)
                last.then_inc(hid_ok, 1)

            pre0 = Sample(0, 0)
            normalise(pre0)
            high_part(pre0)
            exponentials(pre0)
            weights_high(pre0, 0)

            def slot(s):
                more = not s.at_least(N - 1)
                if s.at_least(N):
                    return
                weights_high(s, 1)
                hidden(s, 0)
                residual(s)
                hidden(s, 1)
                hidden(s, 2)
                if more:
                    normalise(s.plus(1))
                hidden(s, 3)
                if more:
                    high_part(s.plus(1))
                hidden(s, 4)
                if more:
                    exponentials(s.plus(1))
                    weights_high(s.plus(1), 0)

            schedule(act, slot)

        @block.vector
        def _(dve):
            link = Link(dve, dve_link)
            nc.vector.memset(padded[:, :, :, :, :, :], 0.0).then_inc(consts_ok, 1)
            nc.vector.memset(ones[:, :], 1.0)
            nc.vector.memset(small[:, :, :], 0.0).then_inc(consts_ok, 1)

            def statistics(t):
                dve.wait_ge(x_in[t.parity], LOAD * (t.pair + 1))
                flat = xin[t.parity][:, :, :].rearrange("p b w -> p (b w)")
                for j in range(STAT):
                    last = nc.vector.bn_stats(stats[t.parity][:, j, :], flat[:, j * SC:(j + 1) * SC])
                link(last)

            def aggregate(t):
                nc.vector.bn_aggr(mv[t.parity][:, :],
                                  stats[t.parity][:, :, :].rearrange("p a b -> p (a b)")).then_inc(mv_ok, 1)

            def deviation(t):
                c = col[t.parity]
                dve.wait_ge(mean_ps, t.number + 1)
                nc.vector.tensor_scalar(c[:, NMEAN:NMEAN + 1], pstat[:, 0:1], -1.0, None, ALU.mult)
                link(nc.vector.tensor_tensor(c[:, DEV:DEV + 1], pstat[:, 0:1], mv[t.parity][:, 0:1], ALU.subtract))
                nc.vector.scalar_tensor_tensor(out=c[:, DVAR:DVAR + 1], in0=c[:, DEV:DEV + 1],
                                               scalar=c[:, DEV:DEV + 1], in1=mv[t.parity][:, 1:2],
                                               op0=ALU.mult, op1=ALU.add).then_inc(dvar_ok, 1)

            def variance(t):
                dve.wait_ge(var_ps, t.number + 1)
                nc.vector.tensor_scalar(col[t.parity][:, VEPS:VEPS + 1], pstat[:, 1:2], EPS, None,
                                        ALU.add).then_inc(veps_ok, 1)

            def pooled_times_gate(t):
                dve.wait_ge(xh_ok, t.number + 1)
                nc.vector.tensor_scalar(gwp[t.parity][:, :], table[:, 0:E],
                                        col[t.parity][:, POOLED:POOLED + 1], None, ALU.mult).then_inc(gwp_ok, 1)

            def softmax_in(t):
                c = col[t.parity]
                dve.wait_ge(gate_ps, t.number + 1)
                link(nc.vector.scalar_tensor_tensor(out=logit[t.parity][:, :], in0=pgate[:, 0:E],
                                                    scalar=1.0 / (H * W), in1=gbias[:, :],
                                                    op0=ALU.mult, op1=ALU.add))
                nc.vector.tensor_reduce(c[:, NMAX:NMAX + 1], logit[t.parity][:, :], AX_X, ALU.max,
                                        negate=True).then_inc(logit_ok, 1)

            def softmax_out(t):
                c = col[t.parity]
                dve.wait_ge(expo_ok, t.number + 1)
                link(nc.vector.reciprocal(c[:, RSUM:RSUM + 1], c[:, ESUM:ESUM + 1]))
                link(nc.vector.tensor_scalar(gate[t.parity][:, 0:E], expo[t.parity][:, :], c[:, RSUM:RSUM + 1], WS,
                                             ALU.mult, ALU.mult))

            def low_part(t):
                dve.wait_ge(hi1_ok, t.number + 1)
                nc.vector.tensor_tensor(a1[t.parity][:, LO, :, 1:1 + W], xh[:, :, :],
                                        a1[t.parity][:, HI, :, 1:1 + W], ALU.subtract).then_inc(lo1_ok, 1)

            def mixture(t):
                c = col[t.parity]
                if t.known(0):
                    dve.wait_ge(bank_ok, 1)
                for e in range(E):
                    ins = nc.vector.scalar_tensor_tensor(
                        out=mix[:, (e + 1) % 2, :, :], in0=bank[:, e, :, :], scalar=gate[t.parity][:, e:e + 1],
                        in1=bank[:, E, :, :] if e == 0 else mix[:, e % 2, :, :],
                        op0=ALU.mult, op1=ALU.add)
                    if e < E - 1:
                        link(ins)
                ins.then_inc(mix_ok, 1)
                dve.wait_ge(mix_ok, t.number + 1)
                mixed = mix[:, E % 2, :, TAPS:TAPS + 1]
                nc.vector.tensor_scalar(c[:, B1:B1 + 1], mixed[:, 0, :], HS / WS, None, ALU.mult)
                nc.vector.scalar_tensor_tensor(out=c[:, RB:RB + 1], in0=mixed[:, 1, :], scalar=1.0 / WS,
                                               in1=c[:, NBIAS:NBIAS + 1], op0=ALU.mult, op1=ALU.add
                                               ).then_inc(bias_ok, 1)

            def weights(t, v):
                dve.wait_ge(whi_ok, t.number * 2 + v + 1)
                st, cr = wts[t.parity][STRAIGHT], wts[t.parity][CROSSED]
                link(nc.vector.tensor_tensor(st[:, v, LO, :], mix[:, E % 2, v, 0:TAPS], st[:, v, HI, :],
                                             ALU.subtract))
                for a, b in ((0, 1), (1, 0)):
                    last = nc.vector.tensor_copy(halves(cr)[a][:, v].rearrange("p a b -> p (a b)"),
                                                 halves(st)[b][:, v].rearrange("p a b -> p (a b)"))
                last.then_inc((w1_ok, w2_ok)[v], 1)

            def hidden_low(s, g):
                dve.wait_ge(hid_ok, s.number * GRP + g + 1)
                for p0, p1, j0, j1 in group_pieces(g):
                    last = nc.vector.tensor_tensor(a2[s.parity][p0:p1, LO, j0:j1, 1:1 + W],
                                                   hid[g_parity(s, g)][p0:p1, j0 - g * SPG:j1 - g * SPG, :],
                                                   a2[s.parity][p0:p1, HI, j0:j1, 1:1 + W], ALU.subtract)
                last.then_inc(lo2_ok, 1)

            def finish(s, g):
                dve.wait_ge(conv2_ps, s.number * GRP + g + 1)
                if g == 0:
                    dve.wait_ge(res_ok, s.number + 1)
                b = slots(g, 0, NB)
                r = res[s.parity][:, b[0]:b[-1] + 1, :]
                nc.vector.scalar_tensor_tensor(
                    out=r, in0=pg[g][:, 0:len(b) * W].rearrange("p (b w) -> p b w", w=W),
                    scalar=1.0 / (WS * HS), in1=r, op0=ALU.mult, op1=ALU.add).then_inc(fin_ok, 1)

            dve.wait_ge(s_in, 16 * 6)
            link(nc.vector.tensor_copy(small[:, 1, :], small[:, 0, :]))
            nc.vector.tensor_copy(small[:, 2:4, :], small[:, 0:2, :]).then_inc(small_ok, 1)
            dve.wait_ge(w_in, 16 * 6)
            for eg in range(2):
                last = nc.vector.tensor_copy(padded[:, 0, eg, :, 1:4, :],
                                             natural[:, 0, eg, :].rearrange("p (c h w) -> p w h c", c=C, h=3))
            last.then_inc(padded_ok, 1)
            dve.wait_ge(ident_ok, 1)
            link(nc.vector.tensor_reduce(pick[:, :], ident[:, :].rearrange("p (g c) -> p c g", g=G), AX_X, ALU.add))
            for g in range(G):
                last = nc.vector.tensor_scalar(avg[:, g * C:(g + 1) * C], pick[:, :], 1.0 / G, None, ALU.mult)
            link(last)
            dve.wait_ge(table_ps, 1)
            link(nc.vector.tensor_copy(table[:, :], pset[:, 0:3 * E + 2]))
            nc.vector.tensor_copy(bank[:, :, :, TAPS:].rearrange("p e v a -> p v (e a)"),
                                  table[:, E:].rearrange("p (v e) -> p v e", v=2)).then_inc(consts_ok, 1)

            pre0 = Sample(0, 0)
            statistics(pre0)
            aggregate(pre0)
            for m in range(4):
                n = 2 * m + 1
                v, eg, part = n // 4, n // 2 % 2, n % 2
                dve.wait_ge(wt_ps, n + 1)
                nc.vector.tensor_copy(bank[:, 4 * eg:4 * eg + 4, v, part * 96:part * 96 + 96]
                                      .rearrange("p e (j o) -> p e j o", j=3),
                                      pg[n % 4][:, 0:3 * P].rearrange("p (j e o) -> p e j o", j=3, e=4)).then_inc(wt_dve, 1)
            deviation(pre0)
            variance(pre0)
            low_part(pre0)
            pooled_times_gate(pre0)
            softmax_in(pre0)
            softmax_out(pre0)
            mixture(pre0)
            weights(pre0, 0)

            def slot(s):
                more = not s.at_least(N - 1)
                live = not s.at_least(N)
                t = s.plus(1)
                if more:
                    statistics(t)
                if live:
                    weights(s, 1)
                if more:
                    aggregate(t)
                if live:
                    hidden_low(s, 0)
                if more:
                    deviation(t)
                if live:
                    hidden_low(s, 1)
                    hidden_low(s, 2)
                if more:
                    variance(t)
                if live:
                    hidden_low(s, 3)
                    hidden_low(s, 4)
                if more:
                    pooled_times_gate(t)
                    low_part(t)
                if s.at_least(1):
                    finish(s.plus(-1), 0)
                if more:
                    softmax_in(t)
                    softmax_out(t)
                    mixture(t)
                if s.at_least(1):
                    finish(s.plus(-1), 1)
                if more:
                    weights(t, 0)
                if s.at_least(1):
                    finish(s.plus(-1), 2)
                    finish(s.plus(-1), 3)
                    finish(s.plus(-1), 4)

            schedule(dve, slot, link, before=2 * 13)

        @block.gpsimd
        def _(pool):
            link = Link(pool, pool_link)
            nc.gpsimd.memset(minus_half[:, :], -0.5)
            link(nc.gpsimd.memset(ident[:, :], 0.0))
            nc.gpsimd.affine_select(out=ident[:, :], in_=ident[:, :], compare_op=ALU.not_equal, fill=1.0,
                                    base=0, pattern=[[-1, P]], channel_multiplier=1).then_inc(ident_ok, 1)
            for straight, shifted in ((a1, c1), (a2, a2)):
                for i in range(2):
                    link(nc.gpsimd.memset(straight[i][:, :, :, 0:RP:RP - 1], 0.0))
                    last = nc.gpsimd.memset(shifted[i][:, :, 0:NS:NS - 1, :], 0.0)
                last.then_inc(pads_ok, 1)
            pool.wait_ge(wt_act, 4)
            pool.wait_ge(wt_dve, 4)
            pool.wait_ge(consts_ok, 3)
            nc.gpsimd.tensor_scalar(bank[:, E, :, :], bank[:, E, :, :], WS, None, ALU.mult).then_inc(bank_ok, 1)

            def coefficients(t):
                c = col[t.parity]
                pool.wait_ge(veps_ok, t.number + 1)
                link(nc.gpsimd.tensor_tensor(c[:, RSTD:RSTD + 1], c[:, VEPS:VEPS + 1], minus_half[:, :], ALU.pow))
                nc.gpsimd.tensor_tensor(c[:, NBIAS:NBIAS + 1], c[:, NMEAN:NMEAN + 1], c[:, RSTD:RSTD + 1],
                                        ALU.mult)
                nc.gpsimd.tensor_scalar(c[:, RS1:RS1 + 1], c[:, RSTD:RSTD + 1], 1.0, None,
                                        ALU.add).then_inc(coef_ok, 1)

            coefficients(Sample(0, 0))

            def slot(s):
                if not s.at_least(N - 1):
                    coefficients(s.plus(1))

            schedule(pool, slot, link, before=2)


_INS = ["x"] + [f"L0_conv_{n}" for n in ("conv1_w", "conv1_b", "conv2_w", "conv2_b", "experts_w1", "experts_b1",
                                         "experts_w2", "experts_b2", "gate_w", "gate_b")]


def kernel(**inputs):
    import numpy as _np
    import concourse.bacc as _bacc
    from concourse import mybir as _mybir
    from concourse.bass_utils import run_bass_kernel_spmd as _run

    nc = _bacc.Bacc("TRN2", target_bir_lowering=False, num_devices=1)
    arrays, args = {}, []
    for name in _INS:
        a = _np.ascontiguousarray(inputs[name])
        arrays[f"in_{name}"] = a
        args.append(nc.dram_tensor(f"in_{name}", a.shape, _mybir.dt.from_np(a.dtype), kind="ExternalInput").ap())
    shape = arrays["in_x"].shape
    args.append(nc.dram_tensor("out_0", shape, _mybir.dt.from_np(arrays["in_x"].dtype), kind="ExternalOutput").ap())
    build(nc, *args)
    r = _run(nc, [arrays], core_ids=[0])
    return r.results[0]["out_0"]
```

```python
from contextlib import ExitStack

import concourse.bass as bass
from concourse import mybir

F32 = mybir.dt.float32
F16 = mybir.dt.float16
ALU = mybir.AluOpType
ACT = mybir.ActivationFunctionType
AX_X = mybir.AxisListType.X

P = 128
EPS = 1e-5
WS = 16.0
HS = 0.25
STRAIGHT, CROSSED = 0, 1
HI, LO = 0, 1
PRODUCTS = ((HI, HI), (LO, HI), (HI, LO))

WSETS = 3
RING = 6
LAPS = 2


class Sample:

    def __init__(self, i, c):
        self.i, self.c = i, c

    def plus(self, n):
        return Sample(self.i, self.c + n)

    @property
    def number(self):
        return self.i * RING + self.c

    @property
    def parity(self):
        return self.c % 2

    @property
    def ring(self):
        return self.c % RING

    @property
    def lap(self):
        return self.i + self.c // RING

    def known(self, value):
        return isinstance(self.i, int) and self.number == value

    def at_least(self, value):
        if not isinstance(self.i, int):
            assert self.c >= value or self.c + (LAPS - 1) * RING < value
        return self.c >= value


def build(nc, x, w1, b1, w2, b2, ew1, eb1, ew2, eb2, gw, gb, out):
    N, C, H, W = x.shape
    E = ew1.shape[0]
    G = P // C
    NB = H // G
    NS = NB + 1
    RP = W + 2
    GRP = 5
    SPG = NS // GRP
    PIX = NB * W
    TAPS = 3 * 2 * C
    E1 = E + 1
    assert G == 4 and NS == GRP * SPG and SPG * W <= 512 and E1 == 8
    STAT = 6
    SC = PIX // STAT
    LOAD = 16 * G
    STORE = 2 * LOAD

    ctx = ExitStack()
    with ctx:
        def sb(name, shape, dt=F32):
            return ctx.enter_context(nc.sbuf_tensor(name, shape, dt))

        def sem(name):
            return ctx.enter_context(nc.semaphore(name))

        img = [sb(f"img{i}", [P, NB, W]) for i in range(RING)]
        xh = sb("xh", [P, NB, W])
        a1 = [sb(f"a1_{i}", [P, 2, NB, RP], F16) for i in range(2)]
        c1 = [sb(f"c1_{i}", [P, 2, NS, RP], F16) for i in range(2)]
        a2 = [sb(f"a2_{i}", [P, 2, NS, RP], F16) for i in range(2)]
        c2 = [sb(f"c2_{i}", [P, 2, NB, RP], F16) for i in range(2)]
        hid = [sb(f"hid{i}", [P, SPG, W]) for i in range(2)]
        natural = sb("natural", [P, 2, 2, C * 9])
        padded = sb("padded", [P, 2, 2, 3, 5, C])
        bank = sb("bank", [P, E1, 2, TAPS + 1])
        mix = sb("mix", [P, 2, 2, TAPS + 1])
        wts = [[sb(f"wts{i}_{k}", [P, 2, 2, TAPS], F16) for k in range(2)] for i in range(WSETS)]
        small = sb("small", [32, G, C])
        table = sb("table", [P, 3 * E + 2])
        gbias = sb("gbias", [P, E])
        ident = sb("ident", [P, P])
        pick = sb("pick", [P, C])
        avg = sb("avg", [P, P])
        ones = sb("ones", [P, P])
        free = sb("free", [1, RING])
        minus_half = sb("minus_half", [P, 1])
        stats = [sb(f"stats{i}", [P, STAT, 6]) for i in range(RING)]
        mv = [sb(f"mv{i}", [P, 2]) for i in range(RING)]
        col = [sb(f"col{i}", [P, 16]) for i in range(RING)]
        logit = [sb(f"logit{i}", [P, E]) for i in range(RING)]
        expo = [sb(f"expo{i}", [P, E]) for i in range(RING)]
        gwp = [sb(f"gwp{i}", [P, E]) for i in range(RING)]
        gate = [sb(f"gate{i}", [P, E]) for i in range(RING)]
        DEV, DVAR, VEPS, NMEAN, RSTD, NBIAS, RS1, RB, B1, POOLED, NMAX, ESUM, RSUM = range(13)

        pg = [ctx.enter_context(nc.psum_tensor(f"pg{i}", [P, 512], F32)) for i in range(GRP)]
        pstat = ctx.enter_context(nc.psum_tensor("pstat", [P, 512], F32))
        pgate = ctx.enter_context(nc.psum_tensor("pgate", [P, 512], F32))
        pset = ctx.enter_context(nc.psum_tensor("pset", [P, 512], F32))

        x_in = [sem(f"x_in{i}") for i in range(RING)]
        crossed1 = [sem(f"crossed1_{i}") for i in range(RING)]
        crossed2 = sem("crossed2")
        stored = [sem(f"stored{i}") for i in range(RING)]
        x0_half = sem("x0_half")
        w_in = [sem(f"w_in{v}") for v in range(2)]
        s_in = sem("s_in")
        ident_ok = sem("ident_ok")
        consts_ok = sem("consts_ok")
        pads_ok = sem("pads_ok")
        small_ok = sem("small_ok")
        table_ps = sem("table_ps")
        padded_ok = [sem(f"padded_ok{v}") for v in range(2)]
        wt_ps = sem("wt_ps")
        wt_act = sem("wt_act")
        wt_dve = sem("wt_dve")
        bank_ok = sem("bank_ok")
        mv_ok = sem("mv_ok")
        mean_ps = sem("mean_ps")
        dvar_ok = sem("dvar_ok")
        var_ps = sem("var_ps")
        veps_ok = sem("veps_ok")
        coef_ok = sem("coef_ok")
        xh_ok = sem("xh_ok")
        hi1_ok = sem("hi1_ok")
        lo1_ok = sem("lo1_ok")
        gwp_ok = sem("gwp_ok")
        gate_ps = sem("gate_ps")
        logit_ok = sem("logit_ok")
        expo_ok = sem("expo_ok")
        bias_ok = sem("bias_ok")
        mix_step = sem("mix_step")
        mix_ok = sem("mix_ok")
        whi_ok = sem("whi_ok")
        w_ok = sem("w_ok")
        res_ok = sem("res_ok")
        conv1_ps = sem("conv1_ps")
        hid_ok = sem("hid_ok")
        lo2_ok = sem("lo2_ok")
        conv2_ps = sem("conv2_ps")
        fin_ok = sem("fin_ok")
        dve_link = sem("dve_link")
        pool_link = sem("pool_link")

        class Link:

            def __init__(self, eng, s):
                self.eng, self.sem, self.base, self.n = eng, s, 0, 0

            def __call__(self, ins):
                ins.then_inc(self.sem, 1)
                self.n += 1
                self.eng.wait_ge(self.sem, self.base + self.n)

        def halves(t):
            return t[0:P // 2], t[P // 2:P]

        def g_parity(s, g):
            return (s.c * GRP + g) % 2

        def group_pieces(g):
            j0, j1 = g * SPG, (g + 1) * SPG
            if g == 0:
                return ((P - C, P, 0, 1), (0, P, 1, j1))
            if g == GRP - 1:
                return ((0, P, j0, j1 - 1), (0, P - C, j1 - 1, j1))
            return ((0, P, j0, j1),)

        def run(step, s, offset, first, *args):
            t = s.plus(offset)
            if not isinstance(t.i, int):
                assert t.c >= first and t.c + (LAPS - 1) * RING < N
                step(t, *args)
            elif first <= t.number < N:
                step(t, *args)

        def schedule(slot, eng, begin, first, last, link=None, per_slot=0):
            for s in range(begin, first):
                slot(Sample(0, s))
            start = link.n if link else 0
            with eng.Fori(0, LAPS) as i:
                if link:
                    link.base, link.n = i * (per_slot * RING) + start, 0
                for c in range(RING):
                    slot(Sample(i, first + c))
                if link:
                    assert link.n == per_slot * RING, link.n
            if link:
                link.base, link.n = start + per_slot * RING * LAPS, 0
            for s in range(first + RING * LAPS, last + 1):
                slot(Sample(0, s))

        block = ctx.enter_context(nc.Block())

        @block.sync
        def _(sp):
            xv = x.rearrange("n c (k g) w -> n g c k w", g=G)
            ov = out.rearrange("n c (k g) w -> n g c k w", g=G)

            def load(t):
                if t.known(0):
                    for arrived, b0 in ((x0_half, 0), (x_in[0], NB // 2)):
                        for g in range(G):
                            sp.dma_start(img[0][g * C:(g + 1) * C, b0:b0 + NB // 2, :],
                                         xv[0, g, :, b0:b0 + NB // 2, :]).then_inc(arrived, 16)
                    return
                if not isinstance(t.i, int) or t.at_least(RING):
                    sp.wait_ge(stored[t.ring], STORE * (t.lap + 1))
                for g in range(G):
                    sp.dma_start(img[t.ring][g * C:(g + 1) * C, :, :],
                                 xv[t.number, g]).then_inc(x_in[t.ring], 16)

            def store(t, half):
                b0, b1, groups = ((0, 3 * SPG, 3), (3 * SPG, NB, GRP))[half]
                sp.wait_ge(fin_ok, t.number * GRP + groups)
                for g in range(G):
                    sp.dma_start(ov[t.number, g, :, b0:b1, :],
                                 img[t.ring][g * C:(g + 1) * C, b0:b1, :]).then_inc(stored[t.ring], 16)

            def cross1(t):
                sp.wait_ge(lo1_ok, t.number + 1)
                for half, d0 in ((0, 0), (1, 1)):
                    sp.dma_start(halves(c1[t.parity])[half][:, :, d0:d0 + NB, :].rearrange("p a b w -> p a (b w)"),
                                 halves(a1[t.parity])[half].rearrange("p a b w -> p a (b w)")
                                 ).then_inc(crossed1[t.ring], 16)

            def load_kernels():
                for v, ew, bw in ((1, ew2, w2), (0, ew1, w1)):
                    kernels = ew.rearrange("e o c h w -> (e o) (c h w)")
                    sp.dma_start(natural[:, v, 0, :], kernels[0:P, :]).then_inc(w_in[v], 16)
                    sp.dma_start(natural[0:(E - 4) * C, v, 1, :], kernels[P:E * C, :]).then_inc(w_in[v], 16)
                    sp.dma_start(natural[(E - 4) * C:P, v, 1, :],
                                 bw.rearrange("o c h w -> o (c h w)")).then_inc(w_in[v], 16)
            load(Sample(0, 0))
            load_kernels()
            load(Sample(0, 1))
            load(Sample(0, 2))

            def slot(s):
                run(load, s, 2, 3)
                run(cross1, s, 0, 0)
                run(store, s, -2, 0, 0)
                run(store, s, -2, 0, 1)

            schedule(slot, sp, -2, 2, 17)
            for b in range(RING):
                sp.wait_ge(stored[b], STORE * (1 + len(range(b, N, RING))))

        @block.tensor
        def _(pe):
            pe.wait_ge(ident_ok, 1)
            def transpose_table():
                pe.wait_ge(small_ok, 1)
                nc.tensor.transpose(pset[:, 0:32], small[:, :, :].rearrange("p g c -> p (g c)"),
                                    ident[0:32, 0:32]).then_inc(table_ps, 1)

            def transpose_kernels(n):
                v, eg, part = 1 - n // 4, n // 2 % 2, n % 2
                if n % 4 == 0:
                    pe.wait_ge(padded_ok[v], 1)
                if n >= 4:
                    pe.wait_ge(wt_act if n % 2 == 0 else wt_dve, (n - 4) // 2 + 1)
                for j in range(3):
                    kw, row = divmod(part * 3 + j, 2)
                    last = nc.tensor.transpose(
                        pg[n % 4][:, j * P:(j + 1) * P],
                        padded[:, v, eg, kw, 1 - row:5 - row, :].rearrange("p h c -> p (h c)"),
                        ident[:, :])
                last.then_inc(wt_ps, 1)

            def mean_over_rows(t):
                pe.wait_ge(mv_ok, t.number + 1)
                nc.tensor.matmul(pstat[:, 0:1], avg[:, :], mv[t.ring][:, 0:1],
                                 start=True, stop=True).then_inc(mean_ps, 1)

            def var_over_rows(t):
                pe.wait_ge(dvar_ok, t.number + 1)
                nc.tensor.matmul(pstat[:, 1:2], avg[:, :], col[t.ring][:, DVAR:DVAR + 1],
                                 start=True, stop=True).then_inc(var_ps, 1)

            def logits(t):
                pe.wait_ge(gwp_ok, t.number + 1)
                nc.tensor.matmul(pgate[:, 0:E], ones[:, :], gwp[t.ring][:, :],
                                 start=True, stop=True).then_inc(gate_ps, 1)

            def group(v, s, g, *sides):
                for image, weight in PRODUCTS:
                    for kw in range(3):
                        for side, (kind, tile, b0, nb, at) in enumerate(sides):
                            last = nc.tensor.matmul(
                                pg[g][side * 64:side * 64 + 64, at:at + nb * W].rearrange("p (b w) -> p b w", w=W),
                                wts[s.c % WSETS][kind][:, v, weight, kw * 64:(kw + 1) * 64],
                                tile[:, image, b0:b0 + nb, kw:kw + W],
                                start=(image, weight, kw) == (HI, HI, 0),
                                stop=(image, weight, kw) == (*PRODUCTS[-1], 2))
                return last

            def conv1_group(s, g):
                if g == 0:
                    pe.wait_ge(w_ok, s.number + 1)
                    pe.wait_ge(lo1_ok, s.number + 1)
                    pe.wait_ge(crossed1[s.ring], 32 * (s.lap + 1))
                if s.at_least(2):
                    pe.wait_ge(fin_ok, (s.number - 2) * GRP + g + 1)
                elif s.at_least(1):
                    pe.wait_ge(hid_ok, g + 1)
                elif g == 0:
                    pe.wait_ge(wt_act, 4)
                    pe.wait_ge(wt_dve, 4)
                lo = g * SPG
                skip = 1 if g == 0 else 0
                group(0, s, g,
                      (STRAIGHT, a1[s.parity], lo - 1 + skip, SPG - skip, skip * W),
                      (CROSSED, c1[s.parity], lo, SPG, 0)).then_inc(conv1_ps, 1)

            def conv2_group(s, g):
                if g == 0:
                    pe.wait_ge(lo2_ok, (s.number + 1) * GRP)
                    pe.wait_ge(crossed2, s.number + 1)
                if s.at_least(N - 1):
                    pe.wait_ge(fin_ok, (s.number - 1) * GRP + g + 1)
                else:
                    pe.wait_ge(hid_ok, (s.number + 1) * GRP + g + 1)
                n = min(SPG, NB - g * SPG)
                group(1, s, g,
                      (CROSSED, c2[s.parity], g * SPG, n, 0),
                      (STRAIGHT, a2[s.parity], g * SPG + 1, n, 0)).then_inc(conv2_ps, 1)

            mean_over_rows(Sample(0, 0))
            transpose_table()
            transpose_kernels(0)
            var_over_rows(Sample(0, 0))
            transpose_kernels(1)
            transpose_kernels(2)
            transpose_kernels(3)
            transpose_kernels(4)
            transpose_kernels(5)
            transpose_kernels(6)
            transpose_kernels(7)
            logits(Sample(0, 0))
            conv1_group(Sample(0, 0), 0)
            conv1_group(Sample(0, 0), 1)
            mean_over_rows(Sample(0, 1))
            var_over_rows(Sample(0, 1))
            conv1_group(Sample(0, 0), 2)
            logits(Sample(0, 1))
            conv1_group(Sample(0, 0), 3)
            mean_over_rows(Sample(0, 2))
            var_over_rows(Sample(0, 2))
            conv1_group(Sample(0, 0), 4)

            def slot(s):
                run(conv1_group, s, 0, 1, 0)
                run(conv1_group, s, 0, 1, 1)
                run(conv1_group, s, 0, 1, 2)
                run(logits, s, 1, 2)
                run(conv1_group, s, 0, 1, 3)
                run(mean_over_rows, s, 2, 3)
                run(conv1_group, s, 0, 1, 4)
                run(conv2_group, s, -1, 0, 0)
                run(var_over_rows, s, 2, 3)
                run(conv2_group, s, -1, 0, 1)
                run(conv2_group, s, -1, 0, 2)
                run(conv2_group, s, -1, 0, 3)
                run(conv2_group, s, -1, 0, 4)

            schedule(slot, pe, -2, 2, 16)

        @block.scalar
        def _(act):
            rows = [(gw, 0), (eb1, E), (b1.rearrange("(a c) -> a c", a=1), 2 * E),
                    (eb2, 2 * E + 1), (b2.rearrange("(a c) -> a c", a=1), 3 * E + 1)]
            act.wait_ge(consts_ok, 2)
            for src, r in rows:
                act.dma_start(small[r:r + src.shape[0], 0, :], src).then_inc(s_in, 16)
            act.dma_start(gbias[:, :], gb.rearrange("(a e) -> a e", a=1).to_broadcast([P, E])).then_inc(s_in, 16)
            def pad_kernels():
                act.wait_ge(w_in[1], 16 * 3)
                act.wait_ge(consts_ok, 1)
                for eg in range(2):
                    last = nc.scalar.copy(padded[:, 1, eg, :, 1:4, :],
                                      natural[:, 1, eg, :].rearrange("p (c h w) -> p w h c", c=C, h=3))
                last.then_inc(padded_ok[1], 1)
            def copy_kernels(n):
                v, eg, part = 1 - n // 4, n // 2 % 2, n % 2
                act.wait_ge(wt_ps, n + 1)
                nc.scalar.copy(bank[:, 4 * eg:4 * eg + 4, v, part * 96:part * 96 + 96]
                               .rearrange("p e (j o) -> p e j o", j=3),
                               pg[n % 4][:, 0:3 * P].rearrange("p (j e o) -> p e j o", j=3, e=4)).then_inc(wt_act, 1)

            def normalise(t):
                c = col[t.ring]
                act.wait_ge(coef_ok, t.number + 1)
                if t.at_least(1):
                    act.wait_ge(lo1_ok, t.number)
                nc.scalar.activation(xh[:, :, :], img[t.ring][:, :, :], ACT.Identity,
                                     bias=c[:, NBIAS:NBIAS + 1], scale=c[:, RSTD:RSTD + 1],
                                     accum_out=c[:, POOLED:POOLED + 1]).then_inc(xh_ok, 1)

            def high_part(t):
                c = col[t.ring]
                if t.at_least(2):
                    act.wait_ge(conv1_ps, (t.number - 1) * GRP)
                else:
                    act.wait_ge(pads_ok, 1)
                nc.scalar.activation(a1[t.parity][:, HI, :, 1:1 + W], img[t.ring][:, :, :], ACT.Identity,
                                     bias=c[:, NBIAS:NBIAS + 1], scale=c[:, RSTD:RSTD + 1]).then_inc(hi1_ok, 1)

            def exponentials(t):
                act.wait_ge(logit_ok, t.number + 1)
                c = col[t.ring]
                nc.scalar.activation(expo[t.ring][:, :], logit[t.ring][:, :], ACT.Exp,
                                     bias=c[:, NMAX:NMAX + 1],
                                     accum_out=c[:, ESUM:ESUM + 1]).then_inc(expo_ok, 1)

            def weights_high(t):
                act.wait_ge(mix_ok, t.number + 1)
                if t.at_least(WSETS):
                    act.wait_ge(conv2_ps, (t.number - WSETS + 1) * GRP)
                nc.scalar.copy(wts[t.c % WSETS][STRAIGHT][:, :, HI, :],
                               mix[:, E % 2, :, 0:TAPS]).then_inc(whi_ok, 1)

            def residual(t):
                c = col[t.ring]
                act.wait_ge(bias_ok, t.number + 1)
                nc.scalar.activation(img[t.ring][:, :, :], img[t.ring][:, :, :], ACT.Identity,
                                     bias=c[:, RB:RB + 1], scale=c[:, RS1:RS1 + 1]).then_inc(res_ok, 1)

            def hidden(s, g):
                c = col[s.ring]
                act.wait_ge(conv1_ps, s.number * GRP + g + 1)
                if not (s.known(0) and g < 2):
                    act.wait_ge(lo2_ok, s.number * GRP + g - 1)
                if g == 0 and s.at_least(2):
                    act.wait_ge(conv2_ps, (s.number - 1) * GRP)
                elif g == 0:
                    act.wait_ge(pads_ok, 2)
                pieces = group_pieces(g)
                dst = ((hid[g_parity(s, g)], None), (a2[s.parity], HI))
                for tile, part in dst:
                    for p0, p1, j0, j1 in pieces:
                        n0 = j0 - g * SPG
                        n1 = j1 - g * SPG
                        o = tile[p0:p1, n0:n1, :] if part is None else tile[p0:p1, part, j0:j1, 1:1 + W]
                        last = nc.scalar.activation(
                            o, pg[g][p0:p1, n0 * W:n1 * W].rearrange("p (b w) -> p b w", w=W), ACT.Relu,
                            bias=c[p0:p1, B1:B1 + 1], scale=HS / WS)
                last.then_inc(hid_ok, 1)

            def cross2(t, half):
                if half == 0:
                    act.wait_ge(lo2_ok, (t.number + 1) * GRP)
                    if t.at_least(2):
                        act.wait_ge(conv2_ps, (t.number - 1) * GRP)
                d, a = (halves(k[t.parity])[half].rearrange("p a b w -> p a (b w)").bitcast(F32) for k in (c2, a2))
                first = (1 - half) * RP // 2
                last = nc.scalar.copy(d, a[:, :, first:first + NB * RP // 2])
                if half == 1:
                    last.then_inc(crossed2, 1)

            pad_kernels()
            copy_kernels(0)
            copy_kernels(2)
            normalise(Sample(0, 0))
            high_part(Sample(0, 0))
            exponentials(Sample(0, 0))
            copy_kernels(4)
            copy_kernels(6)
            weights_high(Sample(0, 0))
            hidden(Sample(0, 0), 0)
            normalise(Sample(0, 1))
            high_part(Sample(0, 1))

            def slot(s):
                run(hidden, s, -1, 0, 4)
                run(normalise, s, 1, 2)
                run(high_part, s, 1, 2)
                run(cross2, s, -1, 0, 0)
                run(hidden, s, 0, 1, 0)
                run(hidden, s, 0, 0, 1)
                run(exponentials, s, 1, 1)
                run(cross2, s, -1, 0, 1)
                run(hidden, s, 0, 0, 2)
                run(hidden, s, 0, 0, 3)
                run(residual, s, 0, 0)
                run(weights_high, s, 1, 1)

            schedule(slot, act, -1, 3, 16)

        @block.vector
        def _(dve):
            link = Link(dve, dve_link)
            nc.vector.memset(padded[:, :, :, :, :, :], 0.0).then_inc(consts_ok, 1)
            nc.vector.memset(ones[:, :], 1.0)
            nc.vector.memset(small[:, :, :], 0.0).then_inc(consts_ok, 1)

            def statistics(t):
                if t.known(0):
                    dve.wait_ge(x0_half, LOAD)
                else:
                    dve.wait_ge(x_in[t.ring], LOAD * (t.lap + 1))
                flat = img[t.ring][:, :, :].rearrange("p b w -> p (b w)")
                for j in range(STAT):
                    if t.known(0) and j==STAT//2:
                        dve.wait_ge(x_in[0], LOAD)
                    last = nc.vector.bn_stats(stats[t.ring][:, j, :], flat[:, j * SC:(j + 1) * SC])
                link(last)

            def aggregate(t):
                nc.vector.bn_aggr(mv[t.ring][:, :],
                                  stats[t.ring][:, :, :].rearrange("p a b -> p (a b)")).then_inc(mv_ok, 1)

            def deviation(t):
                c = col[t.ring]
                dve.wait_ge(mean_ps, t.number + 1)
                nc.vector.tensor_scalar(c[:, NMEAN:NMEAN + 1], pstat[:, 0:1], -1.0, None, ALU.mult)
                link(nc.vector.tensor_tensor(c[:, DEV:DEV + 1], pstat[:, 0:1], mv[t.ring][:, 0:1], ALU.subtract))
                nc.vector.scalar_tensor_tensor(out=c[:, DVAR:DVAR + 1], in0=c[:, DEV:DEV + 1],
                                               scalar=c[:, DEV:DEV + 1], in1=mv[t.ring][:, 1:2],
                                               op0=ALU.mult, op1=ALU.add).then_inc(dvar_ok, 1)

            def variance(t):
                dve.wait_ge(var_ps, t.number + 1)
                nc.vector.tensor_scalar(col[t.ring][:, VEPS:VEPS + 1], pstat[:, 1:2], EPS, None,
                                        ALU.add).then_inc(veps_ok, 1)

            def pooled_times_gate(t):
                dve.wait_ge(xh_ok, t.number + 1)
                nc.vector.tensor_scalar(gwp[t.ring][:, :], table[:, 0:E],
                                        col[t.ring][:, POOLED:POOLED + 1], None, ALU.mult).then_inc(gwp_ok, 1)

            def softmax_in(t):
                c = col[t.ring]
                dve.wait_ge(gate_ps, t.number + 1)
                link(nc.vector.scalar_tensor_tensor(out=logit[t.ring][:, :], in0=pgate[:, 0:E],
                                                    scalar=1.0 / (H * W), in1=gbias[:, :],
                                                    op0=ALU.mult, op1=ALU.add))
                nc.vector.tensor_reduce(c[:, NMAX:NMAX + 1], logit[t.ring][:, :], AX_X, ALU.max,
                                        negate=True).then_inc(logit_ok, 1)

            def softmax_out(t):
                c = col[t.ring]
                dve.wait_ge(expo_ok, t.number + 1)
                link(nc.vector.reciprocal(c[:, RSUM:RSUM + 1], c[:, ESUM:ESUM + 1]))
                link(nc.vector.tensor_scalar(gate[t.ring][:, 0:E], expo[t.ring][:, :], c[:, RSUM:RSUM + 1], WS,
                                             ALU.mult, ALU.mult))

            def low_part(t):
                dve.wait_ge(hi1_ok, t.number + 1)
                nc.vector.tensor_tensor(a1[t.parity][:, LO, :, 1:1 + W], xh[:, :, :],
                                        a1[t.parity][:, HI, :, 1:1 + W], ALU.subtract).then_inc(lo1_ok, 1)

            def mixture(t, e):
                if e == 0 and t.known(0):
                    dve.wait_ge(bank_ok, 1)
                if e > 0:
                    dve.wait_ge(mix_step, t.number * (E - 1) + e)
                nc.vector.scalar_tensor_tensor(
                    out=mix[:, (e + 1) % 2, :, :], in0=bank[:, e, :, :], scalar=gate[t.ring][:, e:e + 1],
                    in1=bank[:, E, :, :] if e == 0 else mix[:, e % 2, :, :],
                    op0=ALU.mult, op1=ALU.add).then_inc(mix_step if e < E - 1 else mix_ok, 1)

            def biases(t):
                dve.wait_ge(mix_ok, t.number + 1)
                c = col[t.ring]
                mixed = mix[:, E % 2, :, TAPS:TAPS + 1]
                nc.vector.tensor_scalar(c[:, B1:B1 + 1], mixed[:, 0, :], HS / WS, None, ALU.mult)
                nc.vector.scalar_tensor_tensor(out=c[:, RB:RB + 1], in0=mixed[:, 1, :], scalar=1.0 / WS,
                                               in1=c[:, NBIAS:NBIAS + 1], op0=ALU.mult, op1=ALU.add
                                               ).then_inc(bias_ok, 1)

            def weights(t):
                dve.wait_ge(whi_ok, t.number + 1)
                st, cr = wts[t.c % WSETS][STRAIGHT], wts[t.c % WSETS][CROSSED]
                link(nc.vector.tensor_tensor(st[:, :, LO, :], mix[:, E % 2, :, 0:TAPS], st[:, :, HI, :],
                                             ALU.subtract))
                for a, b in ((0, 1), (1, 0)):
                    last = nc.vector.tensor_copy(halves(cr)[a].rearrange("p v a b -> p (v a b)"),
                                                 halves(st)[b].rearrange("p v a b -> p (v a b)"))
                last.then_inc(w_ok, 1)

            def hidden_low(s, g):
                dve.wait_ge(hid_ok, s.number * GRP + g + 1)
                for p0, p1, j0, j1 in group_pieces(g):
                    last = nc.vector.tensor_tensor(a2[s.parity][p0:p1, LO, j0:j1, 1:1 + W],
                                                   hid[g_parity(s, g)][p0:p1, j0 - g * SPG:j1 - g * SPG, :],
                                                   a2[s.parity][p0:p1, HI, j0:j1, 1:1 + W], ALU.subtract)
                last.then_inc(lo2_ok, 1)

            def finish(s, g):
                dve.wait_ge(conv2_ps, s.number * GRP + g + 1)
                if g == 0:
                    dve.wait_ge(res_ok, s.number + 1)
                b0, b1 = g * SPG, min((g + 1) * SPG, NB)
                r = img[s.ring][:, b0:b1, :]
                nc.vector.scalar_tensor_tensor(
                    out=r, in0=pg[g][:, 0:(b1 - b0) * W].rearrange("p (b w) -> p b w", w=W),
                    scalar=1.0 / (WS * HS), in1=r, op0=ALU.mult, op1=ALU.add).then_inc(fin_ok, 1)

            def repeat_table():
                dve.wait_ge(s_in, 16 * 6)
                link(nc.vector.tensor_copy(small[:, 1, :], small[:, 0, :]))
                nc.vector.tensor_copy(small[:, 2:4, :], small[:, 0:2, :]).then_inc(small_ok, 1)
            def pad_kernels():
                dve.wait_ge(w_in[0], 16 * 3)
                for eg in range(2):
                    last = nc.vector.tensor_copy(padded[:, 0, eg, :, 1:4, :],
                                             natural[:, 0, eg, :].rearrange("p (c h w) -> p w h c", c=C, h=3))
                last.then_inc(padded_ok[0], 1)
            def averaging():
                dve.wait_ge(ident_ok, 1)
                link(nc.vector.tensor_reduce(pick[:, :], ident[:, :].rearrange("p (g c) -> p c g", g=G), AX_X, ALU.add))
                for g in range(G):
                    last = nc.vector.tensor_scalar(avg[:, g * C:(g + 1) * C], pick[:, :], 1.0 / G, None, ALU.mult)
                link(last)
            def copy_table():
                dve.wait_ge(table_ps, 1)
                link(nc.vector.tensor_copy(table[:, :], pset[:, 0:3 * E + 2]))
                nc.vector.tensor_copy(bank[:, :, :, TAPS:].rearrange("p e v a -> p v (e a)"),
                                  table[:, E:].rearrange("p (v e) -> p v e", v=2)).then_inc(consts_ok, 1)
            def copy_kernels(n):
                v, eg, part = 1 - n // 4, n // 2 % 2, n % 2
                dve.wait_ge(wt_ps, n + 1)
                nc.vector.tensor_copy(bank[:, 4 * eg:4 * eg + 4, v, part * 96:part * 96 + 96]
                                      .rearrange("p e (j o) -> p e j o", j=3),
                                      pg[n % 4][:, 0:3 * P].rearrange("p (j e o) -> p e j o", j=3, e=4)).then_inc(wt_dve, 1)

            averaging()
            statistics(Sample(0, 0))
            repeat_table()
            aggregate(Sample(0, 0))
            pad_kernels()
            deviation(Sample(0, 0))
            variance(Sample(0, 0))
            copy_kernels(1)
            copy_kernels(3)
            copy_table()
            copy_kernels(5)
            pooled_times_gate(Sample(0, 0))
            copy_kernels(7)
            softmax_in(Sample(0, 0))
            low_part(Sample(0, 0))
            softmax_out(Sample(0, 0))
            mixture(Sample(0, 0), 0)
            mixture(Sample(0, 0), 1)
            mixture(Sample(0, 0), 2)
            mixture(Sample(0, 0), 3)
            mixture(Sample(0, 0), 4)
            mixture(Sample(0, 0), 5)
            mixture(Sample(0, 0), 6)
            biases(Sample(0, 0))
            weights(Sample(0, 0))
            statistics(Sample(0, 1))
            aggregate(Sample(0, 1))
            deviation(Sample(0, 1))
            variance(Sample(0, 1))
            statistics(Sample(0, 2))

            def slot(s):
                run(finish, s, -2, 0, 3)
                run(finish, s, -2, 0, 4)
                run(statistics, s, 2, 3)
                run(pooled_times_gate, s, 1, 1)
                run(aggregate, s, 2, 2)
                run(softmax_in, s, 1, 1)
                run(hidden_low, s, 0, 0, 0)
                run(low_part, s, 1, 1)
                run(softmax_out, s, 1, 1)
                run(hidden_low, s, 0, 0, 1)
                run(mixture, s, 1, 1, 0)
                run(mixture, s, 1, 1, 1)
                run(deviation, s, 2, 2)
                run(mixture, s, 1, 1, 2)
                run(mixture, s, 1, 1, 3)
                run(hidden_low, s, 0, 0, 2)
                run(mixture, s, 1, 1, 4)
                run(mixture, s, 1, 1, 5)
                run(mixture, s, 1, 1, 6)
                run(variance, s, 2, 2)
                run(finish, s, -1, 0, 0)
                run(biases, s, 1, 1)
                run(weights, s, 1, 1)
                run(hidden_low, s, 0, 0, 3)
                run(hidden_low, s, 0, 0, 4)
                run(finish, s, -1, 0, 1)
                run(finish, s, -1, 0, 2)

            schedule(slot, dve, -2, 2, 17, link, 6)

        @block.gpsimd
        def _(pool):
            link = Link(pool, pool_link)
            nc.gpsimd.memset(minus_half[:, :], -0.5)
            for b in range(RING):
                nc.gpsimd.memset(free[0:1, b:b + 1], 0.0).then_inc(stored[b], STORE)
            link(nc.gpsimd.memset(ident[:, :], 0.0))
            nc.gpsimd.affine_select(out=ident[:, :], in_=ident[:, :], compare_op=ALU.not_equal, fill=1.0,
                                    base=0, pattern=[[-1, P]], channel_multiplier=1).then_inc(ident_ok, 1)
            for straight, shifted in ((a1, c1), (a2, a2)):
                for i in range(2):
                    link(nc.gpsimd.memset(straight[i][:, :, :, 0:RP:RP - 1], 0.0))
                    last = nc.gpsimd.memset(shifted[i][:, :, 0:NS:NS - 1, :], 0.0)
                last.then_inc(pads_ok, 1)
            def coefficients(t):
                c = col[t.ring]
                pool.wait_ge(veps_ok, t.number + 1)
                link(nc.gpsimd.tensor_tensor(c[:, RSTD:RSTD + 1], c[:, VEPS:VEPS + 1], minus_half[:, :], ALU.pow))
                nc.gpsimd.tensor_tensor(c[:, NBIAS:NBIAS + 1], c[:, NMEAN:NMEAN + 1], c[:, RSTD:RSTD + 1],
                                        ALU.mult)
                nc.gpsimd.tensor_scalar(c[:, RS1:RS1 + 1], c[:, RSTD:RSTD + 1], 1.0, None,
                                        ALU.add).then_inc(coef_ok, 1)

            def scale_shared():
                pool.wait_ge(wt_act, 4)
                pool.wait_ge(wt_dve, 4)
                pool.wait_ge(consts_ok, 3)
                nc.gpsimd.tensor_scalar(bank[:, E, :, :], bank[:, E, :, :], WS, None,
                                        ALU.mult).then_inc(bank_ok, 1)

            coefficients(Sample(0, 0))
            scale_shared()

            def slot(s):
                run(coefficients, s, 2, 1)

            schedule(slot, pool, -1, 2, N - 3, link, 1)


_INS = ["x"] + [f"L0_conv_{n}" for n in ("conv1_w", "conv1_b", "conv2_w", "conv2_b", "experts_w1", "experts_b1",
                                         "experts_w2", "experts_b2", "gate_w", "gate_b")]


def kernel(**inputs):
    import numpy as _np
    import concourse.bacc as _bacc
    from concourse import mybir as _mybir
    from concourse.bass_utils import run_bass_kernel_spmd as _run

    nc = _bacc.Bacc("TRN2", target_bir_lowering=False, num_devices=1)
    arrays, args = {}, []
    for name in _INS:
        a = _np.ascontiguousarray(inputs[name])
        arrays[f"in_{name}"] = a
        args.append(nc.dram_tensor(f"in_{name}", a.shape, _mybir.dt.from_np(a.dtype), kind="ExternalInput").ap())
    shape = arrays["in_x"].shape
    args.append(nc.dram_tensor("out_0", shape, _mybir.dt.from_np(arrays["in_x"].dtype), kind="ExternalOutput").ap())
    build(nc, *args)
    r = _run(nc, [arrays], core_ids=[0])
    return r.results[0]["out_0"]
```

```python
from contextlib import ExitStack

import concourse.bass as bass
from concourse import mybir

F32 = mybir.dt.float32
F16 = mybir.dt.float16
ALU = mybir.AluOpType
ACT = mybir.ActivationFunctionType
AX_X = mybir.AxisListType.X

P = 128
EPS = 1e-5
WS = 16.0
HS = 0.25
STRAIGHT, CROSSED = 0, 1
HI, LO = 0, 1
PRODUCTS = ((HI, HI), (HI, LO), (LO, HI))

WSETS = 3
RING = 6
LAPS = 2
EARLY = 2
WARM = 7


class Sample:

    def __init__(self, i, c):
        self.i, self.c = i, c

    def plus(self, n):
        return Sample(self.i, self.c + n)

    @property
    def number(self):
        return self.i * RING + self.c

    @property
    def parity(self):
        return self.c % 2

    @property
    def ring(self):
        return self.c % RING

    @property
    def lap(self):
        return self.i + self.c // RING

    def known(self, value):
        return isinstance(self.i, int) and self.number == value

    def at_least(self, value):
        if not isinstance(self.i, int):
            assert self.c >= value or self.c + (LAPS - 1) * RING < value
        return self.c >= value


def build(nc, x, w1, b1, w2, b2, ew1, eb1, ew2, eb2, gw, gb, out):
    N, C, H, W = x.shape
    E = ew1.shape[0]
    G = P // C
    NB = H // G
    NS = NB + 1
    RP = W + 2
    GRP = 5
    SPG = NS // GRP
    PIX = NB * W
    TAPS = 3 * 2 * C
    E1 = E + 1
    assert G == 4 and NS == GRP * SPG and SPG * W <= 512 and E1 == 8
    STAT = 6
    SC = PIX // STAT
    LOAD = 16 * G
    STORE = 2 * LOAD

    ctx = ExitStack()
    with ctx:
        def sb(name, shape, dt=F32):
            return ctx.enter_context(nc.sbuf_tensor(name, shape, dt))

        def sem(name):
            return ctx.enter_context(nc.semaphore(name))

        img = [sb(f"img{i}", [P, NB, W]) for i in range(RING)]
        xh = [sb(f"xh{i}", [P, NB, W]) for i in range(2)]
        a1 = [sb(f"a1_{i}", [P, 2, NB, RP], F16) for i in range(2)]
        c1 = [sb(f"c1_{i}", [P, 2, NS, RP], F16) for i in range(2)]
        a2 = [sb(f"a2_{i}", [P, 2, NS, RP], F16) for i in range(2)]
        c2 = [sb(f"c2_{i}", [P, 2, NB, RP], F16) for i in range(2)]
        hid = [sb(f"hid{i}", [P, SPG, W]) for i in range(2)]
        natural = sb("natural", [P, 2, 2, C * 9])
        padded = sb("padded", [P, 2, 2, 3, 5, C])
        bank = sb("bank", [P, E1, 2, TAPS + 1])
        mix = sb("mix", [P, 2, 2, TAPS + 1])
        wts = [[sb(f"wts{i}_{k}", [P, 2, 2, TAPS], F16) for k in range(2)] for i in range(WSETS)]
        small = sb("small", [32, G, C])
        table = sb("table", [P, 3 * E + 2])
        gbias = sb("gbias", [P, E])
        ident = sb("ident", [P, P])
        pick = sb("pick", [P, C])
        same = sb("same", [P, P])
        row = sb("row", [P, 2, G])
        triples = [sb(f"triples{i}", [P, G, 3]) for i in range(2)]
        ones = sb("ones", [P, P])
        free = sb("free", [1, RING])
        minus_half = sb("minus_half", [P, 1])
        stats = [sb(f"stats{i}", [P, STAT, 6]) for i in range(RING)]
        mv = [sb(f"mv{i}", [P, 2]) for i in range(RING)]
        col = [sb(f"col{i}", [P, 16]) for i in range(RING)]
        logit = [sb(f"logit{i}", [P, E]) for i in range(RING)]
        expo = [sb(f"expo{i}", [P, E]) for i in range(RING)]
        gwp = [sb(f"gwp{i}", [P, E]) for i in range(RING)]
        gate = [sb(f"gate{i}", [P, E]) for i in range(RING)]
        NUMBER, VEPS, NMEAN, RSTD, NBIAS, RS1, RB, B1, POOLED, NMAX, ESUM, RSUM, MEAN, VAR = range(14)

        pg = [ctx.enter_context(nc.psum_tensor(f"pg{i}", [P, 512], F32)) for i in range(GRP)]
        pstat = ctx.enter_context(nc.psum_tensor("pstat", [P, 512], F32))
        pgate = ctx.enter_context(nc.psum_tensor("pgate", [P, 512], F32))
        pset = ctx.enter_context(nc.psum_tensor("pset", [P, 512], F32))

        x_in = [sem(f"x_in{i}") for i in range(RING)]
        crossed1 = [sem(f"crossed1_{i}") for i in range(RING)]
        crossed1_high = [sem(f"crossed1_high{i}") for i in range(EARLY)]
        crossed2 = sem("crossed2")
        stored = [sem(f"stored{i}") for i in range(RING)]
        x_half = [sem(f"x_half{i}") for i in range(EARLY)]
        w_in = [sem(f"w_in{v}") for v in range(2)]
        s_in = sem("s_in")
        ident_ok = sem("ident_ok")
        table_ok = sem("table_ok")
        pads_ok = sem("pads_ok")
        small_ok = sem("small_ok")
        table_ps = sem("table_ps")
        padded_ok = [sem(f"padded_ok{v}") for v in range(2)]
        wt_ps = sem("wt_ps")
        wt_act = sem("wt_act")
        wt_dve = sem("wt_dve")
        bank_ok = sem("bank_ok")
        mv_ok = sem("mv_ok")
        rows_ps = sem("rows_ps")
        veps_ok = sem("veps_ok")
        coef_ok = sem("coef_ok")
        xh_ok = sem("xh_ok")
        hi1_ok = sem("hi1_ok")
        lo1_ok = sem("lo1_ok")
        gwp_ok = sem("gwp_ok")
        gate_ps = sem("gate_ps")
        logit_ok = sem("logit_ok")
        expo_ok = sem("expo_ok")
        bias_ok = sem("bias_ok")
        mix_step = sem("mix_step")
        mix_ok = sem("mix_ok")
        whi_ok = sem("whi_ok")
        w_ok = sem("w_ok")
        res_ok = sem("res_ok")
        conv1_ps = sem("conv1_ps")
        hid_ok = sem("hid_ok")
        lo2_ok = sem("lo2_ok")
        conv2_ps = sem("conv2_ps")
        fin_ok = sem("fin_ok")
        dve_link = sem("dve_link")
        pool_link = sem("pool_link")

        class Link:

            def __init__(self, eng, s):
                self.eng, self.sem, self.base, self.n = eng, s, 0, 0

            def __call__(self, ins):
                ins.then_inc(self.sem, 1)
                self.n += 1
                self.eng.wait_ge(self.sem, self.base + self.n)

        def halves(t):
            return t[0:P // 2], t[P // 2:P]

        def g_parity(s, g):
            return (s.c * GRP + g) % 2

        def group_pieces(g):
            j0, j1 = g * SPG, (g + 1) * SPG
            if g == 0:
                return ((P - C, P, 0, 1), (0, P, 1, j1))
            if g == GRP - 1:
                return ((0, P, j0, j1 - 1), (0, P - C, j1 - 1, j1))
            return ((0, P, j0, j1),)

        def early(t):
            return isinstance(t.i, int) and t.number < EARLY

        def run(step, s, offset, first, *args):
            t = s.plus(offset)
            if not isinstance(t.i, int):
                assert t.c >= first and t.c + (LAPS - 1) * RING < N
                step(t, *args)
            elif first <= t.number < N:
                step(t, *args)

        def schedule(slot, eng, begin, first, last, link=None, per_slot=0):
            for s in range(begin, first):
                slot(Sample(0, s))
            start = link.n if link else 0
            with eng.Fori(0, LAPS) as i:
                if link:
                    link.base, link.n = i * (per_slot * RING) + start, 0
                for c in range(RING):
                    slot(Sample(i, first + c))
                if link:
                    assert link.n == per_slot * RING, link.n
            if link:
                link.base, link.n = start + per_slot * RING * LAPS, 0
            for s in range(first + RING * LAPS, last + 1):
                slot(Sample(0, s))

        block = ctx.enter_context(nc.Block())

        @block.sync
        def _(sp):
            xv = x.rearrange("n c (k g) w -> n g c k w", g=G)
            ov = out.rearrange("n c (k g) w -> n g c k w", g=G)

            def load(t):
                if early(t):
                    for arrived, b0 in ((x_half[t.ring], 0), (x_in[t.ring], NB // 2)):
                        for g in range(G):
                            sp.dma_start(img[t.ring][g * C:(g + 1) * C, b0:b0 + NB // 2, :],
                                         xv[t.number, g, :, b0:b0 + NB // 2, :]).then_inc(arrived, 16)
                    return
                if not isinstance(t.i, int) or t.at_least(RING):
                    sp.wait_ge(stored[t.ring], STORE * (t.lap + 1))
                for g in range(G):
                    sp.dma_start(img[t.ring][g * C:(g + 1) * C, :, :],
                                 xv[t.number, g]).then_inc(x_in[t.ring], 16)

            def store(t, half):
                if t.known(N - 1):
                    pieces = (((0, 2), (2, 3)), ((3, 4), (4, GRP)))[half]
                else:
                    pieces = (((0, 3),), ((3, GRP),))[half]
                for g0, g1 in pieces:
                    b0, b1 = g0 * SPG, min(g1 * SPG, NB)
                    sp.wait_ge(fin_ok, t.number * GRP + g1)
                    for g in range(G):
                        sp.dma_start(ov[t.number, g, :, b0:b1, :],
                                     img[t.ring][g * C:(g + 1) * C, b0:b1, :]).then_inc(stored[t.ring], 16)

            def cross1(t):
                if early(t):
                    parts = ((hi1_ok, HI, LO, crossed1_high[t.ring]), (lo1_ok, LO, 2, crossed1[t.ring]))
                else:
                    parts = ((lo1_ok, HI, 2, crossed1[t.ring]),)
                for ready, p0, p1, done in parts:
                    sp.wait_ge(ready, t.number + 1)
                    for half, d0 in ((0, 0), (1, 1)):
                        sp.dma_start(halves(c1[t.parity])[half][:, p0:p1, d0:d0 + NB, :].rearrange("p a b w -> p a (b w)"),
                                     halves(a1[t.parity])[half][:, p0:p1].rearrange("p a b w -> p a (b w)")
                                     ).then_inc(done, 16)

            def load_kernels():
                for v, ew, bw in ((1, ew2, w2), (0, ew1, w1)):
                    kernels = ew.rearrange("e o c h w -> (e o) (c h w)")
                    sp.dma_start(natural[:, v, 0, :], kernels[0:P, :]).then_inc(w_in[v], 16)
                    sp.dma_start(natural[0:(E - 4) * C, v, 1, :], kernels[P:E * C, :]).then_inc(w_in[v], 16)
                    sp.dma_start(natural[(E - 4) * C:P, v, 1, :],
                                 bw.rearrange("o c h w -> o (c h w)")).then_inc(w_in[v], 16)
            load_kernels()
            load(Sample(0, 0))

            def slot(s):
                run(load, s, 2, 1)
                run(cross1, s, 0, 0)
                run(store, s, -2, 0, 0)
                run(store, s, -2, 0, 1)

            schedule(slot, sp, -2, 2, 17)
            for b in range(RING):
                images = len(range(b, N, RING)) + (2 if b == (N - 1) % RING else 1)
                sp.wait_ge(stored[b], STORE * images)

        @block.tensor
        def _(pe):
            pe.wait_ge(ident_ok, 1)

            def transpose_table():
                pe.wait_ge(small_ok, 1)
                nc.tensor.transpose(pset[:, 0:32], small[:, :, :].rearrange("p g c -> p (g c)"),
                                    ident[0:32, 0:32]).then_inc(table_ps, 1)

            def transpose_kernels(n):
                v, eg, part = 1 - n // 4, n // 2 % 2, n % 2
                if n % 4 == 0:
                    pe.wait_ge(padded_ok[v], 1)
                if n >= 4:
                    pe.wait_ge(wt_act if n % 2 == 0 else wt_dve, (n - 4) // 2 + 1)
                for j in range(3):
                    kw, row = divmod(part * 3 + j, 2)
                    last = nc.tensor.transpose(
                        pg[n % 4][:, j * P:(j + 1) * P],
                        padded[:, v, eg, kw, 1 - row:5 - row, :].rearrange("p h c -> p (h c)"),
                        ident[:, :])
                last.then_inc(wt_ps, 1)

            def warm_up():
                for _ in range(WARM):
                    nc.tensor.matmul(pset[:, P:2 * P], ident[:, :], same[:, :], start=True, stop=True)

            def wait_low_part(s):
                pe.wait_ge(lo1_ok, s.number + 1)
                pe.wait_ge(crossed1[s.ring], 32 * (s.lap + 1))

            def gather_rows(t):
                pe.wait_ge(mv_ok, t.number + 1)
                nc.tensor.matmul(pstat[:, 0:3 * G], same[:, :],
                                 triples[t.parity][:, :, :].rearrange("p g a -> p (g a)"),
                                 start=True, stop=True).then_inc(rows_ps, 1)

            def logits(t):
                pe.wait_ge(gwp_ok, t.number + 1)
                nc.tensor.matmul(pgate[:, 0:E], ones[:, :], gwp[t.ring][:, :],
                                 start=True, stop=True).then_inc(gate_ps, 1)

            def group(v, s, g, *sides):
                for image, weight in PRODUCTS:
                    if early(s) and v == 0 and g == 0 and image == LO:
                        wait_low_part(s)
                    for kw in range(3):
                        for side, (kind, tile, b0, nb, at) in enumerate(sides):
                            last = nc.tensor.matmul(
                                pg[g][side * 64:side * 64 + 64, at:at + nb * W].rearrange("p (b w) -> p b w", w=W),
                                wts[s.c % WSETS][kind][:, v, weight, kw * 64:(kw + 1) * 64],
                                tile[:, image, b0:b0 + nb, kw:kw + W],
                                start=(image, weight, kw) == (HI, HI, 0),
                                stop=(image, weight, kw) == (*PRODUCTS[-1], 2))
                return last

            def conv1_group(s, g):
                if g == 0:
                    pe.wait_ge(w_ok, s.number + 1)
                    if early(s):
                        pe.wait_ge(crossed1_high[s.ring], 32)
                    else:
                        wait_low_part(s)
                if s.at_least(2):
                    pe.wait_ge(fin_ok, (s.number - 2) * GRP + g + 1)
                elif s.at_least(1):
                    pe.wait_ge(hid_ok, g + 1)
                elif g == 0:
                    pe.wait_ge(wt_act, 4)
                    pe.wait_ge(wt_dve, 4)
                lo = g * SPG
                skip = 1 if g == 0 else 0
                group(0, s, g,
                      (STRAIGHT, a1[s.parity], lo - 1 + skip, SPG - skip, skip * W),
                      (CROSSED, c1[s.parity], lo, SPG, 0)).then_inc(conv1_ps, 1)

            def conv2_group(s, g):
                if g == 0:
                    pe.wait_ge(lo2_ok, (s.number + 1) * GRP)
                    pe.wait_ge(crossed2, s.number + 1)
                if s.at_least(N - 1):
                    pe.wait_ge(fin_ok, (s.number - 1) * GRP + g + 1)
                else:
                    pe.wait_ge(hid_ok, (s.number + 1) * GRP + g + 1)
                n = min(SPG, NB - g * SPG)
                group(1, s, g,
                      (CROSSED, c2[s.parity], g * SPG, n, 0),
                      (STRAIGHT, a2[s.parity], g * SPG + 1, n, 0)).then_inc(conv2_ps, 1)

            for n in range(6):
                transpose_kernels(n)
            gather_rows(Sample(0, 0))
            transpose_kernels(6)
            transpose_table()
            transpose_kernels(7)
            logits(Sample(0, 0))
            gather_rows(Sample(0, 1))
            logits(Sample(0, 1))
            warm_up()
            conv1_group(Sample(0, 0), 0)
            conv1_group(Sample(0, 0), 1)
            conv1_group(Sample(0, 0), 2)
            gather_rows(Sample(0, 2))
            conv1_group(Sample(0, 0), 3)
            conv1_group(Sample(0, 0), 4)
            conv1_group(Sample(0, 1), 0)
            logits(Sample(0, 2))
            conv1_group(Sample(0, 1), 1)

            def slot(s):
                run(conv1_group, s, 0, 2, 0)
                run(conv1_group, s, 0, 2, 1)
                run(conv1_group, s, 0, 1, 2)
                run(logits, s, 1, 3)
                run(conv1_group, s, 0, 1, 3)
                run(gather_rows, s, 2, 3)
                run(conv1_group, s, 0, 1, 4)
                run(conv2_group, s, -1, 0, 0)
                run(conv2_group, s, -1, 0, 1)
                run(conv2_group, s, -1, 0, 2)
                run(conv2_group, s, -1, 0, 3)
                run(conv2_group, s, -1, 0, 4)

            schedule(slot, pe, -2, 2, 16)

        @block.scalar
        def _(act):
            def copy_kernels(n):
                v, eg, part = 1 - n // 4, n // 2 % 2, n % 2
                act.wait_ge(wt_ps, n + 1)
                nc.scalar.copy(bank[:, 4 * eg:4 * eg + 4, v, part * 96:part * 96 + 96]
                               .rearrange("p e (j o) -> p e j o", j=3),
                               pg[n % 4][:, 0:3 * P].rearrange("p (j e o) -> p e j o", j=3, e=4)).then_inc(wt_act, 1)

            def normalise(t):
                c = col[t.ring]
                act.wait_ge(coef_ok, t.number + 1)
                if t.at_least(2):
                    act.wait_ge(lo1_ok, t.number - 1)
                nc.scalar.activation(xh[t.parity][:, :, :], img[t.ring][:, :, :], ACT.Identity,
                                     bias=c[:, NBIAS:NBIAS + 1], scale=c[:, RSTD:RSTD + 1],
                                     accum_out=c[:, POOLED:POOLED + 1]).then_inc(xh_ok, 1)

            def high_part(t):
                c = col[t.ring]
                if t.at_least(2):
                    act.wait_ge(conv1_ps, (t.number - 1) * GRP)
                else:
                    act.wait_ge(pads_ok, 1)
                nc.scalar.activation(a1[t.parity][:, HI, :, 1:1 + W], img[t.ring][:, :, :], ACT.Identity,
                                     bias=c[:, NBIAS:NBIAS + 1], scale=c[:, RSTD:RSTD + 1]).then_inc(hi1_ok, 1)

            def exponentials(t):
                act.wait_ge(logit_ok, t.number + 1)
                c = col[t.ring]
                nc.scalar.activation(expo[t.ring][:, :], logit[t.ring][:, :], ACT.Exp,
                                     bias=c[:, NMAX:NMAX + 1],
                                     accum_out=c[:, ESUM:ESUM + 1]).then_inc(expo_ok, 1)

            def weights_high(t):
                act.wait_ge(mix_ok, t.number + 1)
                if t.at_least(WSETS):
                    act.wait_ge(conv2_ps, (t.number - WSETS + 1) * GRP)
                nc.scalar.copy(wts[t.c % WSETS][STRAIGHT][:, :, HI, :],
                               mix[:, E % 2, :, 0:TAPS]).then_inc(whi_ok, 1)

            def residual(t):
                c = col[t.ring]
                act.wait_ge(bias_ok, t.number + 1)
                nc.scalar.activation(img[t.ring][:, :, :], img[t.ring][:, :, :], ACT.Identity,
                                     bias=c[:, RB:RB + 1], scale=c[:, RS1:RS1 + 1]).then_inc(res_ok, 1)

            def hidden(s, g):
                c = col[s.ring]
                act.wait_ge(conv1_ps, s.number * GRP + g + 1)
                if not (s.known(0) and g < 2):
                    act.wait_ge(lo2_ok, s.number * GRP + g - 1)
                if g == 0 and s.at_least(2):
                    act.wait_ge(conv2_ps, (s.number - 1) * GRP)
                elif g == 0:
                    act.wait_ge(pads_ok, 2)
                pieces = group_pieces(g)
                dst = ((hid[g_parity(s, g)], None), (a2[s.parity], HI))
                for tile, part in dst:
                    for p0, p1, j0, j1 in pieces:
                        n0 = j0 - g * SPG
                        n1 = j1 - g * SPG
                        o = tile[p0:p1, n0:n1, :] if part is None else tile[p0:p1, part, j0:j1, 1:1 + W]
                        last = nc.scalar.activation(
                            o, pg[g][p0:p1, n0 * W:n1 * W].rearrange("p (b w) -> p b w", w=W), ACT.Relu,
                            bias=c[p0:p1, B1:B1 + 1], scale=HS / WS)
                last.then_inc(hid_ok, 1)

            def cross2(t, half):
                if half == 0:
                    act.wait_ge(lo2_ok, (t.number + 1) * GRP)
                    if t.at_least(2):
                        act.wait_ge(conv2_ps, (t.number - 1) * GRP)
                d, a = (halves(k[t.parity])[half].rearrange("p a b w -> p a (b w)").bitcast(F32) for k in (c2, a2))
                first = (1 - half) * RP // 2
                last = nc.scalar.copy(d, a[:, :, first:first + NB * RP // 2])
                if half == 1:
                    last.then_inc(crossed2, 1)

            copy_kernels(0)
            copy_kernels(2)
            copy_kernels(4)
            copy_kernels(6)
            normalise(Sample(0, 0))
            high_part(Sample(0, 0))
            exponentials(Sample(0, 0))
            normalise(Sample(0, 1))
            weights_high(Sample(0, 0))
            exponentials(Sample(0, 1))
            residual(Sample(0, 0))
            high_part(Sample(0, 1))
            hidden(Sample(0, 0), 0)
            hidden(Sample(0, 0), 1)
            hidden(Sample(0, 0), 2)
            weights_high(Sample(0, 1))
            hidden(Sample(0, 0), 3)
            normalise(Sample(0, 2))
            hidden(Sample(0, 0), 4)
            hidden(Sample(0, 1), 0)
            high_part(Sample(0, 2))
            cross2(Sample(0, 0), 0)
            cross2(Sample(0, 0), 1)
            exponentials(Sample(0, 2))
            hidden(Sample(0, 1), 1)

            def slot(s):
                run(hidden, s, -1, 1, 2)
                run(hidden, s, -1, 1, 3)
                run(normalise, s, 1, 3)
                run(hidden, s, -1, 1, 4)
                run(weights_high, s, 0, 2)
                run(high_part, s, 1, 3)
                run(residual, s, -1, 1)
                run(hidden, s, 0, 2, 0)
                run(hidden, s, 0, 2, 1)
                run(cross2, s, -1, 1, 0)
                run(cross2, s, -1, 1, 1)
                run(exponentials, s, 1, 3)

            schedule(slot, act, -1, 3, 16)

        @block.vector
        def _(dve):
            link = Link(dve, dve_link)
            nc.vector.memset(ones[:, :], 1.0)
            nc.vector.memset(padded[:, :, :, :, 0:5:4, :].rearrange("p v e k h c -> p (v e k) h c"), 0.0)

            def statistics(t):
                if early(t):
                    dve.wait_ge(x_half[t.ring], LOAD)
                else:
                    dve.wait_ge(x_in[t.ring], LOAD * (t.lap + 1))
                flat = img[t.ring][:, :, :].rearrange("p b w -> p (b w)")
                for j in range(STAT):
                    if early(t) and j == STAT // 2:
                        dve.wait_ge(x_in[t.ring], LOAD)
                    last = nc.vector.bn_stats(stats[t.ring][:, j, :], flat[:, j * SC:(j + 1) * SC])
                link(last)

            def aggregate(t):
                link(nc.vector.bn_aggr(mv[t.ring][:, :], stats[t.ring][:, :, :].rearrange("p a b -> p (a b)")))
                nc.vector.tensor_scalar(triples[t.parity][:, :, 1], row[:, 0, :], mv[t.ring][:, 0:1], None, ALU.mult)
                nc.vector.tensor_scalar(triples[t.parity][:, :, 2], row[:, 1, :], mv[t.ring][:, 1:2], None,
                                        ALU.mult).then_inc(mv_ok, 1)

            def channel_moments(t):
                c = col[t.ring]
                dve.wait_ge(rows_ps, t.number + 1)
                nc.vector.tensor_copy(c[:, NUMBER:NUMBER + 1], pstat[:, 0:1])
                link(nc.vector.bn_aggr(c[:, MEAN:VAR + 1], pstat[:, 0:3 * G]))
                nc.vector.tensor_scalar(c[:, NMEAN:NMEAN + 1], c[:, MEAN:MEAN + 1], -1.0, None, ALU.mult)
                nc.vector.tensor_scalar(c[:, VEPS:VEPS + 1], c[:, VAR:VAR + 1], EPS, None,
                                        ALU.add).then_inc(veps_ok, 1)

            def pooled_times_gate(t):
                dve.wait_ge(xh_ok, t.number + 1)
                nc.vector.tensor_scalar(gwp[t.ring][:, :], table[:, 0:E],
                                        col[t.ring][:, POOLED:POOLED + 1], None, ALU.mult).then_inc(gwp_ok, 1)

            def softmax_in(t):
                c = col[t.ring]
                dve.wait_ge(gate_ps, t.number + 1)
                link(nc.vector.scalar_tensor_tensor(out=logit[t.ring][:, :], in0=pgate[:, 0:E],
                                                    scalar=1.0 / (H * W), in1=gbias[:, :],
                                                    op0=ALU.mult, op1=ALU.add))
                nc.vector.tensor_reduce(c[:, NMAX:NMAX + 1], logit[t.ring][:, :], AX_X, ALU.max,
                                        negate=True).then_inc(logit_ok, 1)

            def softmax_out(t):
                c = col[t.ring]
                dve.wait_ge(expo_ok, t.number + 1)
                link(nc.vector.reciprocal(c[:, RSUM:RSUM + 1], c[:, ESUM:ESUM + 1]))
                link(nc.vector.tensor_scalar(gate[t.ring][:, 0:E], expo[t.ring][:, :], c[:, RSUM:RSUM + 1], WS,
                                             ALU.mult, ALU.mult))

            def low_part(t):
                dve.wait_ge(hi1_ok, t.number + 1)
                if t.known(EARLY):
                    dve.wait_ge(lo1_ok, EARLY)
                nc.vector.tensor_tensor(a1[t.parity][:, LO, :, 1:1 + W], xh[t.parity][:, :, :],
                                        a1[t.parity][:, HI, :, 1:1 + W], ALU.subtract).then_inc(lo1_ok, 1)

            def mixture(t, e):
                if e == 0 and t.known(0):
                    dve.wait_ge(bank_ok, 1)
                if e > 0:
                    dve.wait_ge(mix_step, t.number * (E - 1) + e)
                nc.vector.scalar_tensor_tensor(
                    out=mix[:, (e + 1) % 2, :, :], in0=bank[:, e, :, :], scalar=gate[t.ring][:, e:e + 1],
                    in1=bank[:, E, :, :] if e == 0 else mix[:, e % 2, :, :],
                    op0=ALU.mult, op1=ALU.add).then_inc(mix_step if e < E - 1 else mix_ok, 1)

            def biases(t):
                dve.wait_ge(mix_ok, t.number + 1)
                c = col[t.ring]
                mixed = mix[:, E % 2, :, TAPS:TAPS + 1]
                nc.vector.tensor_scalar(c[:, B1:B1 + 1], mixed[:, 0, :], HS / WS, None, ALU.mult)
                nc.vector.scalar_tensor_tensor(out=c[:, RB:RB + 1], in0=mixed[:, 1, :], scalar=1.0 / WS,
                                               in1=c[:, NBIAS:NBIAS + 1], op0=ALU.mult, op1=ALU.add
                                               ).then_inc(bias_ok, 1)

            def weights(t):
                dve.wait_ge(whi_ok, t.number + 1)
                st, cr = wts[t.c % WSETS][STRAIGHT], wts[t.c % WSETS][CROSSED]
                link(nc.vector.tensor_tensor(st[:, :, LO, :], mix[:, E % 2, :, 0:TAPS], st[:, :, HI, :],
                                             ALU.subtract))
                for a, b in ((0, 1), (1, 0)):
                    last = nc.vector.tensor_copy(halves(cr)[a].rearrange("p v a b -> p (v a b)"),
                                                 halves(st)[b].rearrange("p v a b -> p (v a b)"))
                last.then_inc(w_ok, 1)

            def hidden_low(s, g):
                dve.wait_ge(hid_ok, s.number * GRP + g + 1)
                for p0, p1, j0, j1 in group_pieces(g):
                    last = nc.vector.tensor_tensor(a2[s.parity][p0:p1, LO, j0:j1, 1:1 + W],
                                                   hid[g_parity(s, g)][p0:p1, j0 - g * SPG:j1 - g * SPG, :],
                                                   a2[s.parity][p0:p1, HI, j0:j1, 1:1 + W], ALU.subtract)
                last.then_inc(lo2_ok, 1)

            def finish(s, g):
                dve.wait_ge(conv2_ps, s.number * GRP + g + 1)
                if g == 0:
                    dve.wait_ge(res_ok, s.number + 1)
                b0, b1 = g * SPG, min((g + 1) * SPG, NB)
                r = img[s.ring][:, b0:b1, :]
                nc.vector.scalar_tensor_tensor(
                    out=r, in0=pg[g][:, 0:(b1 - b0) * W].rearrange("p (b w) -> p b w", w=W),
                    scalar=1.0 / (WS * HS), in1=r, op0=ALU.mult, op1=ALU.add).then_inc(fin_ok, 1)

            def repeat_table():
                dve.wait_ge(s_in, 16 * 6)
                link(nc.vector.tensor_copy(small[:, 1, :], small[:, 0, :]))
                nc.vector.tensor_copy(small[:, 2:4, :], small[:, 0:2, :]).then_inc(small_ok, 1)

            def pad_kernels(v):
                dve.wait_ge(w_in[v], 16 * 3)
                for eg in range(2):
                    last = nc.vector.tensor_copy(padded[:, v, eg, :, 1:4, :],
                                             natural[:, v, eg, :].rearrange("p (c h w) -> p w h c", c=C, h=3))
                last.then_inc(padded_ok[v], 1)

            def row_constants():
                dve.wait_ge(ident_ok, 1)
                link(nc.vector.tensor_reduce(pick[:, :], ident[:, :].rearrange("p (g c) -> p c g", g=G), AX_X, ALU.add))
                for g in range(G):
                    nc.vector.tensor_copy(same[:, g * C:(g + 1) * C], pick[:, :])
                link(nc.vector.tensor_reduce(row[:, 0, :], ident[:, :].rearrange("p (g c) -> p g c", g=G), AX_X, ALU.add))
                link(nc.vector.tensor_scalar(row[:, 1, :], row[:, 0, :], float(PIX), None, ALU.mult))
                for i in range(2):
                    last = nc.vector.tensor_copy(triples[i][:, :, 0], row[:, 1, :])
                link(last)

            def copy_table():
                dve.wait_ge(table_ps, 1)
                link(nc.vector.tensor_copy(table[:, :], pset[:, 0:3 * E + 2]))
                nc.vector.tensor_copy(bank[:, :, :, TAPS:].rearrange("p e v a -> p v (e a)"),
                                  table[:, E:].rearrange("p (v e) -> p v e", v=2)).then_inc(table_ok, 1)

            def copy_kernels(n):
                v, eg, part = 1 - n // 4, n // 2 % 2, n % 2
                dve.wait_ge(wt_ps, n + 1)
                nc.vector.tensor_copy(bank[:, 4 * eg:4 * eg + 4, v, part * 96:part * 96 + 96]
                                      .rearrange("p e (j o) -> p e j o", j=3),
                                      pg[n % 4][:, 0:3 * P].rearrange("p (j e o) -> p e j o", j=3, e=4)).then_inc(wt_dve, 1)

            pad_kernels(1)
            copy_kernels(1)
            copy_kernels(3)
            pad_kernels(0)
            row_constants()
            copy_kernels(5)
            statistics(Sample(0, 0))
            aggregate(Sample(0, 0))
            repeat_table()
            channel_moments(Sample(0, 0))
            copy_table()
            copy_kernels(7)
            statistics(Sample(0, 1))
            pooled_times_gate(Sample(0, 0))
            aggregate(Sample(0, 1))
            softmax_in(Sample(0, 0))
            softmax_out(Sample(0, 0))
            mixture(Sample(0, 0), 0)
            channel_moments(Sample(0, 1))
            mixture(Sample(0, 0), 1)
            mixture(Sample(0, 0), 2)
            mixture(Sample(0, 0), 3)
            mixture(Sample(0, 0), 4)
            mixture(Sample(0, 0), 5)
            pooled_times_gate(Sample(0, 1))
            mixture(Sample(0, 0), 6)
            softmax_in(Sample(0, 1))
            biases(Sample(0, 0))
            weights(Sample(0, 0))
            softmax_out(Sample(0, 1))
            mixture(Sample(0, 1), 0)
            mixture(Sample(0, 1), 1)
            mixture(Sample(0, 1), 2)
            statistics(Sample(0, 2))
            mixture(Sample(0, 1), 3)
            mixture(Sample(0, 1), 4)
            aggregate(Sample(0, 2))
            hidden_low(Sample(0, 0), 0)
            mixture(Sample(0, 1), 5)
            mixture(Sample(0, 1), 6)
            hidden_low(Sample(0, 0), 1)
            channel_moments(Sample(0, 2))
            biases(Sample(0, 1))
            hidden_low(Sample(0, 0), 2)
            weights(Sample(0, 1))
            hidden_low(Sample(0, 0), 3)
            pooled_times_gate(Sample(0, 2))
            hidden_low(Sample(0, 0), 4)
            statistics(Sample(0, 3))
            hidden_low(Sample(0, 1), 0)
            aggregate(Sample(0, 3))
            softmax_in(Sample(0, 2))
            low_part(Sample(0, 2))
            softmax_out(Sample(0, 2))
            mixture(Sample(0, 2), 0)
            channel_moments(Sample(0, 3))
            hidden_low(Sample(0, 1), 1)
            finish(Sample(0, 0), 0)
            mixture(Sample(0, 2), 1)
            hidden_low(Sample(0, 1), 2)
            mixture(Sample(0, 2), 2)
            hidden_low(Sample(0, 1), 3)
            mixture(Sample(0, 2), 3)
            mixture(Sample(0, 2), 4)
            mixture(Sample(0, 2), 5)
            mixture(Sample(0, 2), 6)
            biases(Sample(0, 2))
            finish(Sample(0, 0), 1)
            weights(Sample(0, 2))
            hidden_low(Sample(0, 1), 4)
            finish(Sample(0, 0), 2)
            finish(Sample(0, 0), 3)
            pooled_times_gate(Sample(0, 3))

            def slot(s):
                run(statistics, s, 2, 4)
                run(finish, s, -2, 0, 4)
                run(aggregate, s, 2, 4)
                run(hidden_low, s, 0, 2, 0)
                run(low_part, s, 1, 3)
                run(softmax_in, s, 1, 3)
                run(softmax_out, s, 1, 3)
                run(mixture, s, 1, 3, 0)
                run(channel_moments, s, 2, 4)
                run(hidden_low, s, 0, 2, 1)
                run(mixture, s, 1, 3, 1)
                run(mixture, s, 1, 3, 2)
                run(mixture, s, 1, 3, 3)
                run(mixture, s, 1, 3, 4)
                run(mixture, s, 1, 3, 5)
                run(hidden_low, s, 0, 2, 2)
                run(mixture, s, 1, 3, 6)
                run(biases, s, 1, 3)
                run(pooled_times_gate, s, 2, 4)
                run(weights, s, 1, 3)
                run(finish, s, -1, 1, 0)
                run(hidden_low, s, 0, 2, 3)
                run(hidden_low, s, 0, 2, 4)
                run(finish, s, -1, 1, 1)
                run(finish, s, -1, 1, 2)
                run(finish, s, -1, 1, 3)

            schedule(slot, dve, -2, 2, 17, link, 7)

        @block.gpsimd
        def _(pool):
            link = Link(pool, pool_link)
            nc.gpsimd.memset(minus_half[:, :], -0.5)
            for b in range(RING):
                nc.gpsimd.memset(free[0:1, b:b + 1], 0.0).then_inc(stored[b], STORE)
            link(nc.gpsimd.memset(small[:, :, :], 0.0))
            link(nc.gpsimd.memset(ident[:, :], 0.0))
            nc.gpsimd.affine_select(out=ident[:, :], in_=ident[:, :], compare_op=ALU.not_equal, fill=1.0,
                                    base=0, pattern=[[-1, P]], channel_multiplier=1).then_inc(ident_ok, 1)
            rows = [(gw, 0), (eb1, E), (b1.rearrange("(a c) -> a c", a=1), 2 * E),
                    (eb2, 2 * E + 1), (b2.rearrange("(a c) -> a c", a=1), 3 * E + 1)]
            for src, r in rows:
                nc.gpsimd.dma_start(small[r:r + src.shape[0], 0, :], src).then_inc(s_in, 16)
            nc.gpsimd.dma_start(gbias[:, :], gb.rearrange("(a e) -> a e", a=1).to_broadcast([P, E])).then_inc(s_in, 16)
            for straight, shifted in ((a1, c1), (a2, a2)):
                for i in range(2):
                    link(nc.gpsimd.memset(straight[i][:, :, :, 0:RP:RP - 1], 0.0))
                    last = nc.gpsimd.memset(shifted[i][:, :, 0:NS:NS - 1, :], 0.0)
                last.then_inc(pads_ok, 1)

            def coefficients(t):
                c = col[t.ring]
                pool.wait_ge(veps_ok, t.number + 1)
                link(nc.gpsimd.tensor_tensor(c[:, RSTD:RSTD + 1], c[:, VEPS:VEPS + 1], minus_half[:, :], ALU.pow))
                nc.gpsimd.tensor_tensor(c[:, NBIAS:NBIAS + 1], c[:, NMEAN:NMEAN + 1], c[:, RSTD:RSTD + 1],
                                        ALU.mult)
                nc.gpsimd.tensor_scalar(c[:, RS1:RS1 + 1], c[:, RSTD:RSTD + 1], 1.0, None,
                                        ALU.add).then_inc(coef_ok, 1)

            def scale_shared():
                pool.wait_ge(wt_act, 4)
                pool.wait_ge(wt_dve, 4)
                pool.wait_ge(table_ok, 1)
                nc.gpsimd.tensor_scalar(bank[:, E, :, :], bank[:, E, :, :], WS, None,
                                        ALU.mult).then_inc(bank_ok, 1)

            def low_part(t, b0, b1):
                if b0 == 0:
                    pool.wait_ge(hi1_ok, t.number + 1)
                    if not t.known(0):
                        pool.wait_ge(lo1_ok, t.number)
                last = nc.gpsimd.tensor_tensor(a1[t.parity][:, LO, b0:b1, 1:1 + W], xh[t.parity][:, b0:b1, :],
                                               a1[t.parity][:, HI, b0:b1, 1:1 + W], ALU.subtract)
                if b1 == NB:
                    last.then_inc(lo1_ok, 1)

            coefficients(Sample(0, 0))
            scale_shared()
            low_part(Sample(0, 0), 0, NB // 2)
            coefficients(Sample(0, 1))
            low_part(Sample(0, 0), NB // 2, NB)
            low_part(Sample(0, 1), 0, NB)

            def slot(s):
                run(coefficients, s, 2, 2)

            schedule(slot, pool, 0, 2, N - 3, link, 1)


_INS = ["x"] + [f"L0_conv_{n}" for n in ("conv1_w", "conv1_b", "conv2_w", "conv2_b", "experts_w1", "experts_b1",
                                         "experts_w2", "experts_b2", "gate_w", "gate_b")]


def kernel(**inputs):
    import numpy as _np
    import concourse.bacc as _bacc
    from concourse import mybir as _mybir
    from concourse.bass_utils import run_bass_kernel_spmd as _run

    nc = _bacc.Bacc("TRN2", target_bir_lowering=False, num_devices=1)
    arrays, args = {}, []
    for name in _INS:
        a = _np.ascontiguousarray(inputs[name])
        arrays[f"in_{name}"] = a
        args.append(nc.dram_tensor(f"in_{name}", a.shape, _mybir.dt.from_np(a.dtype), kind="ExternalInput").ap())
    shape = arrays["in_x"].shape
    args.append(nc.dram_tensor("out_0", shape, _mybir.dt.from_np(arrays["in_x"].dtype), kind="ExternalOutput").ap())
    build(nc, *args)
    r = _run(nc, [arrays], core_ids=[0])
    return r.results[0]["out_0"]
```
